# Optimizing a Trainium2 kernel written in Bass

```python
import numpy as np
import jax
import jax.numpy as jnp

def _softmax(x, axis=-1):
    return jax.nn.softmax(x, axis=axis)
def _gelu(x):
    return jax.nn.gelu(x, approximate=True)
def _silu(x):
    return jax.nn.silu(x)
def _sigmoid(x):
    return jax.nn.sigmoid(x)
def _layernorm(x, axis=-1, eps=1e-5):
    m = jnp.mean(x, axis=axis, keepdims=True)
    v = jnp.var(x, axis=axis, keepdims=True)
    return (x - m) / jnp.sqrt(v + eps)
def _scatter_add(tgt, idx, src, axis=0):
    return tgt.at[idx].add(src)
def _segment_sum(src, seg, n):
    return jax.ops.segment_sum(src, seg, n)

kernel_name = 'mk_metaformer_d1_conv_nchw256_f237a0'

def setup_inputs(seed: int = 0):
    np.random.seed(seed)
    _w = jnp.asarray
    def _rec_inputs():
        import jax
        import jax.numpy as jnp
        _gk = jax.random.key(seed)
        x = -0.0002928 + 1 * jax.random.normal(jax.random.fold_in(_gk, 1), (4, 256, 64, 64), jnp.float32)
        return x
    x = _rec_inputs()
    def _L0_conv_setup():
        import jax, jax.numpy as jnp
        from jax import lax
        import numpy as np
        B_, C_, H_, W_ = (4, 256, 64, 64)
        DM = C_ // 4
        DI = 2 * DM
        NS = 16
        KC = 4
        RK = max(1, DM // 16)
        EPS = 1e-05

        def layernorm(x, g, b):
            m = jnp.mean(x, -1, keepdims=True)
            v = jnp.mean(jnp.square(x - m), -1, keepdims=True)
            return (x - m) * lax.rsqrt(v + EPS) * g + b

        def mamba(x, W_in, W_conv, b_conv, W_xproj, W_dt, b_dt, A_log, D_par, W_outp):
            Bt, L, _ = x.shape
            xz = x @ W_in.T
            xc, z = (xz[..., :DI], xz[..., DI:])
            xt = jnp.transpose(xc, (0, 2, 1))
            xt = lax.conv_general_dilated(xt, W_conv, (1,), [(KC - 1, 0)], feature_group_count=DI)
            xc = jax.nn.silu(jnp.transpose(xt + b_conv[None, :, None], (0, 2, 1)))
            x_dbl = xc @ W_xproj.T
            dt = jax.nn.softplus(x_dbl[..., :RK] @ W_dt.T + b_dt)
            Bm = x_dbl[..., RK:RK + NS]
            Cm = x_dbl[..., RK + NS:]
            A = -jnp.exp(A_log)
            a = jnp.exp(dt[..., None] * A)
            bx = dt[..., None] * Bm[:, :, None, :] * xc[..., None]

            def step(h, inp):
                a_t, b_t, c_t = inp
                h = a_t * h + b_t
                y = jnp.einsum('bdn,bn->bd', h, c_t)
                return (h, y)
            h0 = jnp.zeros((Bt, DI, NS), x.dtype)
            _, ys = lax.scan(step, h0, (jnp.swapaxes(a, 0, 1), jnp.swapaxes(bx, 0, 1), jnp.swapaxes(Cm, 0, 1)))
            y = jnp.swapaxes(ys, 0, 1) + xc * D_par
            y = y * jax.nn.silu(z)
            return y @ W_outp.T
        key = jax.random.key(seed)
        ks = jax.random.split(key, 16)
        r = lambda i, shape, s=0.02: jax.random.normal(ks[i], shape, jnp.float32) * s
        return dict(x=jax.random.normal(ks[0], (B_, C_, H_, W_), jnp.float32), g_norm=jnp.ones((C_,), jnp.float32), b_norm=jnp.zeros((C_,), jnp.float32), g_norm1=jnp.ones((DM,), jnp.float32), b_norm1=jnp.zeros((DM,), jnp.float32), W_in=r(1, (2 * DI, DM)), W_conv=r(2, (DI, 1, KC), 0.1), b_conv=r(3, (DI,)), W_xproj=r(4, (RK + 2 * NS, DI)), W_dt=r(5, (DI, RK), 0.1), b_dt=r(6, (DI,)), A_log=jnp.tile(jnp.log(jnp.arange(1, NS + 1, dtype=jnp.float32)), (DI, 1)), D_par=jnp.ones((DI,), jnp.float32), W_outp=r(7, (DM, DI)), skip_scale=jnp.ones((1,), jnp.float32), W_fc1=r(8, (4 * DM, DM)), b_fc1=jnp.zeros((4 * DM,), jnp.float32), W_fc2=r(9, (DM, 4 * DM)), b_fc2=jnp.zeros((DM,), jnp.float32), W_out=r(10, (C_, C_)), bn_g=jnp.ones((C_,), jnp.float32), bn_b=jnp.zeros((C_,), jnp.float32), bn_mean=jnp.zeros((C_,), jnp.float32), bn_var=jnp.ones((C_,), jnp.float32))
    _L0_conv_all = _L0_conv_setup()
    _L0_conv_in = {k: v for k, v in _L0_conv_all.items() if k in ('g_norm', 'b_norm', 'g_norm1', 'b_norm1', 'W_in', 'W_conv', 'b_conv', 'W_xproj', 'W_dt', 'b_dt', 'A_log', 'D_par', 'W_outp', 'skip_scale', 'W_fc1', 'b_fc1', 'W_fc2', 'b_fc2', 'W_out', 'bn_g', 'bn_b', 'bn_mean', 'bn_var', )}
    del _L0_conv_all

    def _L0_ffn_setup():
        import jax, jax.numpy as jnp
        import numpy as np
        NUM_EXPERTS = 8
        TOP_K = 2
        B, S, D = (8, 8192, 256)

        def _moe(tokens, router_w, w1, b1, w2, b2):
            N = tokens.shape[0]
            E = router_w.shape[0]
            logits = tokens.astype(jnp.float32) @ router_w.astype(jnp.float32).T
            probs = jax.nn.softmax(logits, axis=-1)
            rw, re = jax.lax.top_k(probs, TOP_K)
            if TOP_K > 1:
                rw = rw / jnp.maximum(rw.sum(-1, keepdims=True), 1e-12)
            rw = rw.astype(tokens.dtype)
            combine = jnp.zeros((N, E), tokens.dtype).at[jnp.arange(N)[:, None], re].set(rw)
            out = tokens
            for e in range(E):
                h = jax.nn.gelu(tokens @ w1[e] + b1[e], approximate=False)
                y = h @ w2[e] + b2[e]
                out = out + combine[:, e:e + 1] * y
            return out
        key = jax.random.key(seed)
        ks = jax.random.split(key, 4)
        scale = 1.0 / np.sqrt(D).astype(np.float32)
        return {'input_embeddings': jax.random.normal(ks[0], (B, S, D), jnp.float32), 'router_w': jax.random.normal(ks[1], (NUM_EXPERTS, D), jnp.float32) * scale, 'w1': jax.random.normal(ks[2], (NUM_EXPERTS, D, D), jnp.float32) * scale, 'b1': jnp.zeros((NUM_EXPERTS, D), jnp.float32), 'w2': jax.random.normal(ks[3], (NUM_EXPERTS, D, D), jnp.float32) * scale, 'b2': jnp.zeros((NUM_EXPERTS, D), jnp.float32)}
    _L0_ffn_all = _L0_ffn_setup()
    _L0_ffn_in = {k: v for k, v in _L0_ffn_all.items() if k in ('router_w', 'w1', 'b1', 'w2', 'b2', )}
    del _L0_ffn_all

    return {
        "x": x,
        "L0_conv_g_norm": _L0_conv_in["g_norm"],
        "L0_conv_b_norm": _L0_conv_in["b_norm"],
        "L0_conv_g_norm1": _L0_conv_in["g_norm1"],
        "L0_conv_b_norm1": _L0_conv_in["b_norm1"],
        "L0_conv_W_in": _L0_conv_in["W_in"],
        "L0_conv_W_conv": _L0_conv_in["W_conv"],
        "L0_conv_b_conv": _L0_conv_in["b_conv"],
        "L0_conv_W_xproj": _L0_conv_in["W_xproj"],
        "L0_conv_W_dt": _L0_conv_in["W_dt"],
        "L0_conv_b_dt": _L0_conv_in["b_dt"],
        "L0_conv_A_log": _L0_conv_in["A_log"],
        "L0_conv_D_par": _L0_conv_in["D_par"],
        "L0_conv_W_outp": _L0_conv_in["W_outp"],
        "L0_conv_skip_scale": _L0_conv_in["skip_scale"],
        "L0_conv_W_fc1": _L0_conv_in["W_fc1"],
        "L0_conv_b_fc1": _L0_conv_in["b_fc1"],
        "L0_conv_W_fc2": _L0_conv_in["W_fc2"],
        "L0_conv_b_fc2": _L0_conv_in["b_fc2"],
        "L0_conv_W_out": _L0_conv_in["W_out"],
        "L0_conv_bn_g": _L0_conv_in["bn_g"],
        "L0_conv_bn_b": _L0_conv_in["bn_b"],
        "L0_conv_bn_mean": _L0_conv_in["bn_mean"],
        "L0_conv_bn_var": _L0_conv_in["bn_var"],
        "L0_ffn_router_w": _L0_ffn_in["router_w"],
        "L0_ffn_w1": _L0_ffn_in["w1"],
        "L0_ffn_b1": _L0_ffn_in["b1"],
        "L0_ffn_w2": _L0_ffn_in["w2"],
        "L0_ffn_b2": _L0_ffn_in["b2"],
    }

def reference(x, L0_conv_g_norm, L0_conv_b_norm, L0_conv_g_norm1, L0_conv_b_norm1, L0_conv_W_in, L0_conv_W_conv, L0_conv_b_conv, L0_conv_W_xproj, L0_conv_W_dt, L0_conv_b_dt, L0_conv_A_log, L0_conv_D_par, L0_conv_W_outp, L0_conv_skip_scale, L0_conv_W_fc1, L0_conv_b_fc1, L0_conv_W_fc2, L0_conv_b_fc2, L0_conv_W_out, L0_conv_bn_g, L0_conv_bn_b, L0_conv_bn_mean, L0_conv_bn_var, L0_ffn_router_w, L0_ffn_w1, L0_ffn_b1, L0_ffn_w2, L0_ffn_b2):
    import jax
    import jax.numpy as jnp
    def _L0_conv_ref(x, g_norm, b_norm, g_norm1, b_norm1, W_in, W_conv, b_conv, W_xproj, W_dt, b_dt, A_log, D_par, W_outp, skip_scale, W_fc1, b_fc1, W_fc2, b_fc2, W_out, bn_g, bn_b, bn_mean, bn_var):
        import jax, jax.numpy as jnp
        from jax import lax
        import numpy as np
        B_, C_, H_, W_ = (4, 256, 64, 64)
        DM = C_ // 4
        DI = 2 * DM
        NS = 16
        KC = 4
        RK = max(1, DM // 16)
        EPS = 1e-05

        def layernorm(x, g, b):
            m = jnp.mean(x, -1, keepdims=True)
            v = jnp.mean(jnp.square(x - m), -1, keepdims=True)
            return (x - m) * lax.rsqrt(v + EPS) * g + b

        def mamba(x, W_in, W_conv, b_conv, W_xproj, W_dt, b_dt, A_log, D_par, W_outp):
            Bt, L, _ = x.shape
            xz = x @ W_in.T
            xc, z = (xz[..., :DI], xz[..., DI:])
            xt = jnp.transpose(xc, (0, 2, 1))
            xt = lax.conv_general_dilated(xt, W_conv, (1,), [(KC - 1, 0)], feature_group_count=DI)
            xc = jax.nn.silu(jnp.transpose(xt + b_conv[None, :, None], (0, 2, 1)))
            x_dbl = xc @ W_xproj.T
            dt = jax.nn.softplus(x_dbl[..., :RK] @ W_dt.T + b_dt)
            Bm = x_dbl[..., RK:RK + NS]
            Cm = x_dbl[..., RK + NS:]
            A = -jnp.exp(A_log)
            a = jnp.exp(dt[..., None] * A)
            bx = dt[..., None] * Bm[:, :, None, :] * xc[..., None]

            def step(h, inp):
                a_t, b_t, c_t = inp
                h = a_t * h + b_t
                y = jnp.einsum('bdn,bn->bd', h, c_t)
                return (h, y)
            h0 = jnp.zeros((Bt, DI, NS), x.dtype)
            _, ys = lax.scan(step, h0, (jnp.swapaxes(a, 0, 1), jnp.swapaxes(bx, 0, 1), jnp.swapaxes(Cm, 0, 1)))
            y = jnp.swapaxes(ys, 0, 1) + xc * D_par
            y = y * jax.nn.silu(z)
            return y @ W_outp.T
        B, C, H, W = x.shape
        L = H * W
        x_flat = jnp.transpose(x.reshape(B, C, L), (0, 2, 1))
        x_norm = layernorm(x_flat, g_norm, b_norm)
        chunks = x_norm.reshape(B, L, 4, DM)
        xs = jnp.transpose(chunks, (2, 0, 1, 3)).reshape(4 * B, L, DM)
        ym = mamba(xs, W_in, W_conv, b_conv, W_xproj, W_dt, b_dt, A_log, D_par, W_outp)
        yn = layernorm(ym, g_norm1, b_norm1)
        yn = jax.nn.gelu(yn @ W_fc1.T + b_fc1, approximate=False) @ W_fc2.T + b_fc2
        ym = yn + skip_scale * xs
        ym = ym.reshape(4, B, L, DM)
        xi = jnp.transpose(ym, (1, 3, 0, 2)).reshape(B, C, H, W)
        y = jnp.einsum('bchw,oc->bohw', xi, W_out)
        scale = bn_g * lax.rsqrt(bn_var + EPS)
        y = y * scale[None, :, None, None] + (bn_b - bn_mean * scale)[None, :, None, None]
        return jax.nn.silu(y)

    def _L0_ffn_ref(input_embeddings, router_w, w1, b1, w2, b2):
        import jax, jax.numpy as jnp
        import numpy as np
        NUM_EXPERTS = 8
        TOP_K = 2
        B, S, D = (8, 8192, 256)

        def _moe(tokens, router_w, w1, b1, w2, b2):
            N = tokens.shape[0]
            E = router_w.shape[0]
            logits = tokens.astype(jnp.float32) @ router_w.astype(jnp.float32).T
            probs = jax.nn.softmax(logits, axis=-1)
            rw, re = jax.lax.top_k(probs, TOP_K)
            if TOP_K > 1:
                rw = rw / jnp.maximum(rw.sum(-1, keepdims=True), 1e-12)
            rw = rw.astype(tokens.dtype)
            combine = jnp.zeros((N, E), tokens.dtype).at[jnp.arange(N)[:, None], re].set(rw)
            out = tokens
            for e in range(E):
                h = jax.nn.gelu(tokens @ w1[e] + b1[e], approximate=False)
                y = h @ w2[e] + b2[e]
                out = out + combine[:, e:e + 1] * y
            return out
        b, s, d = input_embeddings.shape
        tokens = input_embeddings.reshape(b * s, d)
        return _moe(tokens, router_w, w1, b1, w2, b2).reshape(b, s, d)

    def _gn(v, G=32, eps=1e-5):
        B_, C_, H_, W_ = v.shape
        g = v.reshape(B_, G, C_ // G, H_, W_)
        m = jnp.mean(g, axis=(2, 3, 4), keepdims=True)
        s = jnp.var(g, axis=(2, 3, 4), keepdims=True)
        return ((g - m) / jnp.sqrt(s + eps)).reshape(v.shape)

    def _ln_c(v, eps=1e-6):
        m = jnp.mean(v, axis=1, keepdims=True)
        s = jnp.var(v, axis=1, keepdims=True)
        return (v - m) / jnp.sqrt(s + eps)

    def _ln_t(v, eps=1e-5):
        m = jnp.mean(v, axis=-1, keepdims=True)
        s = jnp.var(v, axis=-1, keepdims=True)
        return (v - m) / jnp.sqrt(s + eps)

    def _to_tokens(v):
        B_, C_, H_, W_ = v.shape
        return v.reshape(B_, C_, H_ * W_).transpose(0, 2, 1)
    def _from_tokens(t, like):
        B_, C_, H_, W_ = like.shape
        return t.transpose(0, 2, 1).reshape(B_, C_, H_, W_)

    x = x + _L0_conv_ref(_ln_c(x), L0_conv_g_norm, L0_conv_b_norm, L0_conv_g_norm1, L0_conv_b_norm1, L0_conv_W_in, L0_conv_W_conv, L0_conv_b_conv, L0_conv_W_xproj, L0_conv_W_dt, L0_conv_b_dt, L0_conv_A_log, L0_conv_D_par, L0_conv_W_outp, L0_conv_skip_scale, L0_conv_W_fc1, L0_conv_b_fc1, L0_conv_W_fc2, L0_conv_b_fc2, L0_conv_W_out, L0_conv_bn_g, L0_conv_bn_b, L0_conv_bn_mean, L0_conv_bn_var)
    t = _to_tokens(x)
    t = t + _L0_ffn_ref(_ln_t(t), L0_ffn_router_w, L0_ffn_w1, L0_ffn_b1, L0_ffn_w2, L0_ffn_b2)
    x = _from_tokens(t, x)
    return x


_drawn_inputs = setup_inputs


def setup_inputs(seed=0):
    import zlib

    import numpy as np

    out = dict(_drawn_inputs(seed))
    spreads = {'L0_conv_g_norm': (1.0, 0.2),
     'L0_conv_b_norm': (0.0, 0.285),
     'L0_conv_g_norm1': (1.0, 0.6),
     'L0_conv_b_norm1': (0.0, 0.8),
     'L0_conv_D_par': (1.0, 0.6),
     'L0_conv_b_fc1': (0.0, 0.712),
     'L0_conv_b_fc2': (0.0, 0.303),
     'L0_conv_bn_g': (1.0, 0.2),
     'L0_conv_bn_b': (0.0, 0.1),
     'L0_conv_bn_mean': (0.0, 0.1),
     'L0_conv_bn_var': (1.0, 0.2),
     'L0_ffn_b1': (0.0, 0.328),
     'L0_ffn_b2': (0.0, 0.1)}
    factors = {'L0_conv_W_in': 8.0,
     'L0_conv_W_conv': 8.0,
     'L0_conv_b_conv': 8.0,
     'L0_conv_W_xproj': 8.0,
     'L0_conv_W_dt': 8.0,
     'L0_conv_b_dt': 8.0,
     'L0_conv_A_log': 8.0,
     'L0_conv_W_outp': 8.0,
     'L0_conv_W_fc1': 8.0,
     'L0_conv_W_fc2': 5.244}
    for name, (base, spread) in spreads.items():
        noise = np.random.default_rng([zlib.crc32(name.encode()), seed]).standard_normal(out[name].shape)
        drawn = base * np.exp(spread * noise) if base else spread * noise
        out[name] = jnp.asarray(drawn.astype(out[name].dtype))
    for name, factor in factors.items():
        out[name] = (out[name] * factor).astype(out[name].dtype)
    return out
```

```python
from contextlib import ExitStack

import concourse.bass as bass
from concourse import mybir

F32 = mybir.dt.float32
BF16 = mybir.dt.bfloat16
U32 = mybir.dt.uint32
ALU = mybir.AluOpType
ACT = mybir.ActivationFunctionType
AX_X = mybir.AxisListType.X

P = 128
B, C, H, W = 4, 256, 64, 64
L = H * W
T = 512
KT = C // P
TILES = B * L // T
PER_IMAGE = L // T
CH = 4
DM = C // CH
DI = 2 * DM
NS = 16
KC = 4
RK = 4
UNITS = DI * NS // P
JU = P // NS
NE = 8
PARTS = 3
RING = 8
TOPK_STEPS = 22
LN_EPS = 1e-5
LNC_EPS = 1e-6
HEAD_ADD = LNC_EPS * LN_EPS / (1.0 + LN_EPS)
HEAD_SCALE = (1.0 + LN_EPS) ** -0.5
EXP_CAP = 2.0 ** 60

SMALL = dict(conv=KC, b_conv=1, b_dt=1, D=1, g=KT, b=KT, g1=1, b1=1, b_fc1=2, b_fc2=1, skip=1,
             bn_g=KT, bn_b=KT, bn_mean=KT, bn_var=KT, moe_b1=NE * 2, A_log=UNITS,
             A=UNITS, g_head=KT, bn_s=KT, bn_t=KT, bn_ns=KT, bn_nt=KT, bn_v=KT, one=1, eps=1, head_add=1)
LOADED = sum(list(SMALL.values())[:17])
COL, _at = {}, 0
for _name, _n in SMALL.items():
    COL[_name] = _at
    _at += _n
NSMALL = _at

def prep(c):
    return -1 if c == 3 else 0


def prev(c):
    return 1 if c == 0 else 0


LATE = {0: 1, 1: 1, 2: 0, 3: 0}
_prepc = [(c, prep(c)) for c in range(CH)]
_prevc = [(c, prev(c)) for c in range(CH)]
_unit = [((c, u), 0) for c in range(CH) for u in range(UNITS)]
_fc1 = [("F", h, m) for h in range(2) for m in range(2)]


def _ga():
    out = []
    for c in range(CH):
        names = {0: ["X", "Z", "outp", "var", "DT", "B", "C"] + _fc1,
                 1: ["X", "Z", "wout0", "wout1", "DT", "B", "C", "tvar"],
                 2: ["X", "Z", "hvar", "outp", "var", "DT", "B", "C"] + _fc1 + [("h", e) for e in range(4)],
                 3: ["X", "Z", "DT", "B", "C"] + [("h", e) for e in range(4, 8)]}[c]
        for n in names:
            if n in ("X", "Z", "DT", "B", "C"):
                lag = prep(c)
            elif isinstance(n, tuple) and n[0] == "h" or n in ("wout0", "wout1", "tvar"):
                lag = 1
            elif n == "hvar":
                lag = -1
            else:
                lag = LATE[c]
            out.append(((c, n), lag))
    return out


_gd = [((1, "fc2"), 1), ((1, "mean"), 1), ((1, "router"), 1), ((1, "combT"), 1), ((2, "hmean"), -1)] \
    + [((2, ("bc", e)), 1) for e in range(4)] + [((3, "fc2"), 0)] + [((3, ("bc", e)), 1) for e in range(4, 8)]
_pairs = [(0, 1), (2, 0)]
_h0 = [(e, 1) for e in range(NE)]
_m = [(m, 1) for m in range(KT)]
EVENTS = dict(
    bcast=_unit, yred=[((c, k), lag if k == "prev" else 0) for c, lag in _prevc for k in ("prev", 0, 1, 2)],
    ga_full=_ga(), gd_full=_gd, gh_full=_h0, moe_full=[(0, 2), (1, 2)],
    ga_evac=_ga(), gh_evac=_h0, exp=_unit, halo=_prepc, neg_exp=_prepc, ln_z=_prepc,
    gate_z=_prepc, ln_x=_prepc, gate_x=_prepc, ln_o=[(0, 1)], gate_o=[(0, 1)], rstd=_pairs, rstd_h=[(0, -1)],
    rstd_t=[(0, 1)], sp_exp=_prepc, sp_ln=_prepc,
    hi=_prepc, mid=_prepc, yn_aff=_pairs, skip_in=[(0, 0), (1, 0)], tail_sq=[(0, 1)], head_sq=[(0, -1)],
    xs=[(0, -1)], topk_exp=[(0, 1)],
    gd_evac=_gd, bx=_unit, scan=_unit, conv=[((c, k), lag) for c, lag in _prepc for k in range(KC - 1)],
    yd=_prevc, cap_z=_prepc, cap_x=_prepc, cap_o=[(0, 1)], sp_max=_prepc, sp_round=_prepc, xc=_prepc, sp_sum=_prepc, dt=_prepc, rest=_prepc, lo=_prepc,
    o=[(0, 1)], tn=[(0, 1)], xn=[(0, -1)], topk=[(k, 1) for k in range(TOPK_STEPS)], moe_evac=[(0, 2), (1, 2)],
    saved=_unit, prod=_unit, yg=_prevc, zs=_prepc, sp_err=_prepc, dtx=_prepc,
    yn=_pairs, x1=[(0, 1)], fin=[(0, 1)],
    xt=[(0, -1)], xr=[(0, 1)], stored=[(0, 2), (1, 2)],
    shuffle0=[((c, k), lag) for c, lag in _prepc if c % 2 == 1 for k in range(PARTS * 4)],
    shuffle1=[((c, k), lag) for c, lag in _prepc if c % 2 == 0 for k in range(PARTS * 4)],
)
DMA_COUNTED = ("xt", "xr", "stored", "shuffle0", "shuffle1")
FIRST, LAST = -1, TILES + 1
LOOP = (3, TILES - 1)


def on(lag, i):
    return not isinstance(i, int) or 0 <= i - lag < TILES


def _in_round(name, i):
    return [k for k, lag in EVENTS[name] if on(lag, i)]


def _before(name, i):
    return sum(len(_in_round(name, j)) for j in range(FIRST, i))


def count(name, i, key=None, back=0):
    n = len(EVENTS[name])
    unit = 16 if name in DMA_COUNTED else 1
    if isinstance(i, int):
        keys = _in_round(name, i - back)
        if key is None:
            return _before(name, i) * unit
        return (_before(name, i - back) + keys.index(key) + 1) * unit if key in keys else 0
    lags = {lag for _, lag in EVENTS[name]}
    assert not back or 2 not in lags or lags == {2}
    index = 0 if key is None else [k for k, _ in EVENTS[name]].index(key) + 1
    constant = _before(name, LOOP[0]) + index - n * back - n * LOOP[0]
    assert n * LOOP[0] + constant > 0
    return i * (n * unit) + constant * unit


def previous(name, i, key):
    return count(name, i, key) - (16 if name in DMA_COUNTED else 1)


def build(nc, x, small, wx, wz, wdtl, wdtr, wb, wc, wo, wf1, wf2, wout, w1, w2, b2, router,
          mean256, mean64, red, iota, sel, sele, ident, out):
    with ExitStack() as ctx:
        def sb(name, shape, dt=F32):
            return ctx.enter_context(nc.sbuf_tensor(name, shape, dt))

        def bank(name):
            return ctx.enter_context(nc.psum_tensor(name, [P, T], F32))

        sem = {name: ctx.enter_context(nc.semaphore(name)) for name in EVENTS}
        ready = ctx.enter_context(nc.semaphore("ready"))
        derived = ctx.enter_context(nc.semaphore("derived"))
        gate = ctx.enter_context(nc.semaphore("gate"))
        setup_mm = ctx.enter_context(nc.semaphore("setup_mm"))
        setup_act = ctx.enter_context(nc.semaphore("setup_act"))
        setup_dve = ctx.enter_context(nc.semaphore("setup_dve"))

        small_s = sb("small_s", [P, NSMALL])
        wx_s, wz_s = sb("wx_s", [P, 2, P]), sb("wz_s", [P, 2, P])
        wdtl_s, wdtr_s, wdt_s = sb("wdtl_s", [RK, P]), sb("wdtr_s", [RK, P]), sb("wdt_s", [P, P])
        wb_s, wc_s = sb("wb_s", [P, P]), sb("wc_s", [P, P])
        wo_s, wof_s = sb("wo_s", [P, DM]), sb("wof_s", [P, 2, P])
        wf1_s, wf2_s = sb("wf1_s", [P, 2, C]), sb("wf2_s", [P, 2, 2, P])
        wout_s = sb("wout_s", [P, KT, C])
        w1_s, w2_s = sb("w1_s", [P, NE, KT, C]), sb("w2_s", [P, NE, KT, C])
        b2_s, router_s = sb("b2_s", [PARTS * NE, C]), sb("router_s", [P, KT, NE])
        mean256_s, mean64_s = sb("mean256_s", [P, P]), sb("mean64_s", [P, P])
        red_s, iota_s = sb("red_s", [P, 4, 32]), sb("iota_s", [P, 4, NE])
        sel_s = sb("sel_s", [PARTS * 32, 4, P], BF16)
        sele_s, ident_s = sb("sele_s", [PARTS * NE, NE, P], BF16), sb("ident_s", [P, P], BF16)
        wo_mean = sb("wo_mean", [P, 1])

        def col(name, k=0, n=1):
            return small_s[:, COL[name] + k:COL[name] + k + n]

        state = sb("state", [P, (PER_IMAGE + 1) * CH * UNITS])
        halo = sb("halo", [P, (PER_IMAGE + 1) * CH * (KC - 1)])

        xn, xs = sb("xn_s", [P, KT, T]), sb("xs_s", [P, KT, T])
        sq2, rs2 = sb("sq2", [P, KT, T]), sb("rs2", [P, T])
        xh, acc = sb("xh", [P, T + KC - 1]), sb("acc", [P, T])
        zc, ez, ex = sb("zc", [P, T]), sb("ez", [P, T]), sb("ex", [P, T])
        v, ev, lnu, dr = zc, ez, ex, acc
        xcs, zs = sb("xcs", [P, 2, T]), sb("zs_s", [P, 2, T])
        bs, cs = sb("bs", [P, 2, T]), sb("cs", [P, 2, T])
        v2 = sb("v2", [P, 2, T])
        part = [sb(n, [P, 2, T], BF16) for n in ("hi_s", "mid_s", "lo_s")]
        pd = [sb(f"pd{k}", [PARTS * 32, 2, 4, T], BF16) for k in range(2)]
        a = sb("a", [P, 2, T])
        h = sb("h", [P, RING, T])
        yg = sb("yg_s", [P, 2, T])
        yn, gl = sb("yn_s", [P, T]), sb("gl", [P, 2, 2, T])
        skip = sb("skip_s", [P, KT, T])
        oc, eo = gl[:, 0, :, :], gl[:, 1, :, :]
        x1, tn, fin = (sb(n, [P, KT, T]) for n in ("x1_s", "tn_s", "fin_s"))
        hc = sb("hc", [P, NE, 2, T])
        lg, mx, comb, cmp = sb("lg", [P, 4, NE]), sb("mx", [P, 4, 8]), sb("comb", [P, 4, NE]), sb("cmp", [P, 2, 4, NE])
        ix, ixf, pr = sb("ix", [P, 4, 8], U32), sb("ixf", [P, 4, 2]), sb("pr", [P, 4, 4])
        c24 = sb("c24", [P, 4, PARTS * NE], BF16)
        combT, combTf = sb("combT", [PARTS * NE, T], BF16), sb("combTf", [PARTS * NE, T])

        pa, pb = [bank(f"pa{k}") for k in range(2)], [bank(f"pb{k}") for k in range(2)]
        py, ga, gd, gh = bank("py"), bank("ga"), bank("gd"), bank("gh")
        gdt = gd[0:PARTS * NE, 0:T // 2].bitcast(BF16)

        loads = [(small_s[:, 0:LOADED], small), (wx_s, wx), (wz_s, wz), (wdtl_s, wdtl), (wdtr_s, wdtr),
                 (wb_s, wb), (wc_s, wc), (wo_s, wo), (wf1_s, wf1), (wf2_s, wf2), (wout_s, wout), (w1_s, w1),
                 (w2_s, w2), (b2_s, b2), (router_s, router), (mean256_s, mean256), (mean64_s, mean64),
                 (red_s, red), (iota_s, iota), (sel_s, sel), (sele_s, sele), (ident_s, ident)]
        READY = 16 * len(loads) + 1

        def met(name, n):
            return (sem[name], n) if not isinstance(n, int) or n > 0 else (derived, 1)

        def after(name, i, key, back=0):
            return met(name, count(name, i, key, back))

        def free(name, i, key):
            return met(name, previous(name, i, key))

        def rounds(eng, one):
            for i in range(FIRST, LOOP[0]):
                one(i)
            with eng.Fori(*LOOP) as i:
                one(i)
            for i in range(LOOP[1], LAST + 1):
                one(i)

        def group(u):
            q, r = u % 4, u // 4
            return q, r, 4 * q + r

        block = ctx.enter_context(nc.Block())

        @block.sync
        def _(sp):
            for dst, src in loads:
                sp.dma_start(dst if isinstance(dst, bass.AP) else dst[:], src).then_inc(ready, 16)

            def one(i):
                if on(1, i):
                    sp.wait_ge(*after("fin", i, 0, back=1))
                    sp.dma_start(x1[:], tile(x, i - 1)).then_inc(sem["xr"], 16)
                if on(-1, i):
                    sp.wait_ge(*after("xs", i, 0, back=1))
                    sp.dma_start(xn[:], tile(x, i + 1)).then_inc(sem["xt"], 16)
                for c in range(CH):
                    if on(prep(c), i):
                        cn = (c + 1) % CH
                        for k, what in enumerate(("hi", "mid", "lo")):
                            sp.wait_ge(*after(what, i, c))
                            for q in range(4):
                                sp.dma_start(pd[cn % 2][32 * k:32 * k + 32, :, q, :],
                                             part[k][32 * q:32 * q + 32, :, :]).then_inc(sem[f"shuffle{cn % 2}"], 16)
                    if c < 2 and on(2, i):
                        sp.wait_ge(*after("moe_evac", i, c))
                        sp.dma_start(tile(out, i - 2)[:, c, :], fin[:, c, :]).then_inc(sem["stored"], 16)

            def tile(dram, j):
                return dram[j] if isinstance(j, int) else dram[bass.ds(j, 1)].rearrange("a p k t -> (a p) k t")

            rounds(sp, one)
            sp.wait_ge(sem["stored"], 16 * KT * TILES)

        @block.tensor
        def _(pe):
            mm = nc.tensor.matmul
            pe.wait_ge(ready, READY)
            mm(ga[:, 0:P], wdtl_s[:], wdtr_s[:], start=True, stop=True).then_inc(setup_mm, 1)
            pe.wait_ge(derived, 1)

            def one(i):
                def bcast(c, u):
                    q, r, _ = group(u)
                    n = c * UNITS + u
                    if u == 0:
                        pe.wait_ge(*after(f"shuffle{c % 2}", i, ((c - 1) % CH, PARTS * 4 - 1), back=1 if c == 0 else 0))
                    if n >= 2:
                        pe.wait_ge(*after("scan", i, divmod(n - 2, UNITS)))
                    else:
                        pe.wait_ge(*after("scan", i, (CH - 1, UNITS - 2 + n), back=1))
                    mm(pa[n % 2][:], sel_s[:, r, :], pd[c % 2][:, 0, q, :], start=True, stop=True)
                    mm(pb[n % 2][:], sel_s[:, r, :], pd[c % 2][:, 1, q, :], start=True, stop=True).then_inc(sem["bcast"], 1)

                def reduce(c, k):
                    if k == "prev":
                        cc, kk = (c - 1) % CH, 3
                        pe.wait_ge(*after("prod", i, (cc, UNITS - 1), back=1 if c == 0 else 0))
                    else:
                        cc, kk = c, k
                        pe.wait_ge(*after("prod", i, (c, 4 * k + 3)))
                        if k == 0:
                            pe.wait_ge(*after("yd", i, c))
                    for q in range(4):
                        n = cc * UNITS + 4 * kk + q
                        ins = mm(py[32 * q:32 * q + 32, :], red_s[:, kk, :], h[:, n % RING, :], start=(kk == 0), stop=(kk == 3))
                    ins.then_inc(sem["yred"], 1)

                def to_act(c, name, pieces):
                    pe.wait_ge(*free("ga_evac", i, (c, name)))
                    for k, (w, r) in enumerate(pieces):
                        ins = mm(ga[:], w, r, start=(k == 0), stop=(k == len(pieces) - 1))
                    ins.then_inc(sem["ga_full"], 1)

                def to_dve(c, name, pieces):
                    pe.wait_ge(*free("gd_evac", i, (c, name)))
                    for k, (w, r) in enumerate(pieces):
                        ins = mm(gd[:], w, r, start=(k == 0), stop=(k == len(pieces) - 1))
                    ins.then_inc(sem["gd_full"], 1)

                def experts_down(m, ks, first=False, last=False):
                    if first:
                        if m == 0:
                            pe.wait_ge(*after("gh_evac", i, NE - 1, back=1))
                            pe.wait_ge(*after("gd_evac", i, (3, ("bc", NE - 1)), back=1))
                        else:
                            pe.wait_ge(*after("moe_evac", i, 0))
                        mm(gh[:], b2_s[:, m * P:m * P + P], combTf[:], start=True, stop=False)
                    for n in ks:
                        e, k = divmod(n, 2)
                        ins = mm(gh[:], w2_s[:, e, k, m * P:m * P + P], hc[:, e, k, :], start=False, stop=(n == 15))
                    if last:
                        ins.then_inc(sem["moe_full"], 1)

                def experts_up(c):
                    for e in range(4 * (c - 2), 4 * (c - 2) + 4):
                        if e == 0:
                            pe.wait_ge(*after("tn", i, 0))
                            pe.wait_ge(*after("moe_evac", i, 1))
                        else:
                            pe.wait_ge(*after("gh_evac", i, e - 1))
                        for k in range(KT):
                            ins = mm(gh[:], w1_s[:, e, k, 0:P], tn[:, k, :], start=(k == 0), stop=(k == KT - 1))
                        ins.then_inc(sem["gh_full"], 1)
                        to_act(c, ("h", e), [(w1_s[:, e, k, P:2 * P], tn[:, k, :]) for k in range(KT)])
                        to_dve(c, ("bc", e), [(sele_s[:, e, :], combT[:])])

                for c in range(CH):
                    cn, par = (c + 1) % CH, (c + 1) % 2
                    ready_ = on(prep(c), i)
                    for u in range(UNITS):
                        if on(0, i):
                            bcast(c, u)
                        if ready_:
                            if u == 0:
                                if c == 3:
                                    pe.wait_ge(*after("xs", i, 0))
                                elif c == 0:
                                    pe.wait_ge(*after("xs", i, 0, back=1))
                                to_act(c, "X", [(wx_s[:, cn % 2, :], xs[:, cn // 2, :])])
                            if u == 3:
                                to_act(c, "Z", [(wz_s[:, cn % 2, :], xs[:, cn // 2, :])])
                            if u == 10:
                                pe.wait_ge(*after("xc", i, c))
                                to_act(c, "DT", [(wdt_s[:], xcs[:, par, :])])
                            if u == 11:
                                to_act(c, "B", [(wb_s[:], xcs[:, par, :])])
                            if u == 12:
                                to_act(c, "C", [(wc_s[:], xcs[:, par, :])])
                        if on(LATE[c], i):
                            if c in (0, 2) and u == 5:
                                pe.wait_ge(*after("yg", i, c))
                                to_act(c, "outp", [(wof_s[:, k, :], yg[:, k, :]) for k in range(2)])
                            if c in (0, 2) and u == 8:
                                pe.wait_ge(*after("ga_evac", i, (c, "outp")))
                                to_act(c, "var", [(mean64_s[:], sq2[:, 0, :])])
                            if c in (1, 3) and u == 1:
                                pe.wait_ge(*after("ga_evac", i, (c - 1, ("F", 1, 1))))
                                to_dve(c, "fc2", [(wf2_s[:, k, hh, :], gl[:, hh, k, :]) for hh in range(2) for k in range(2)])
                        if c == 1 and on(1, i):
                            if u == 4:
                                pe.wait_ge(*after("gd_evac", i, (1, "fc2")))
                            if u in (4, 6):
                                m = (u - 4) // 2
                                to_act(c, f"wout{m}", [(wout_s[:, k, m * P:m * P + P], skip[:, k, :]) for k in range(KT)])
                            if u == 13:
                                pe.wait_ge(*after("x1", i, 0))
                                to_dve(c, "mean", [(mean256_s[:], x1[:, k, :]) for k in range(KT)])
                        if c == 2 and on(-1, i):
                            if u == 1:
                                pe.wait_ge(*after("xt", i, 0))
                                to_dve(c, "hmean", [(mean256_s[:], xn[:, k, :]) for k in range(KT)])
                            if u == 4:
                                pe.wait_ge(*after("head_sq", i, 0))
                                to_act(c, "hvar", [(mean256_s[:], sq2[:, k, :]) for k in range(KT)])
                        if u % 4 == 2:
                            if u == 2:
                                if on(prev(c), i):
                                    reduce(c, "prev")
                            elif on(0, i):
                                reduce(c, u // 4 - 1)
                    if c == 1 and on(1, i):
                        pe.wait_ge(*after("tail_sq", i, 0))
                        to_act(c, "tvar", [(mean256_s[:], sq2[:, k, :]) for k in range(KT)])
                    if c < 2 and on(2, i):
                        experts_down(c, range(0, 8), first=True)
                    if c == 0 or c == 2:
                        if on(LATE[c], i):
                            pe.wait_ge(*after("yn_aff", i, c))
                            for hh in range(2):
                                for m in range(2):
                                    to_act(c, ("F", hh, m), [(wf1_s[:, hh, m * P:m * P + P], yn[:])])
                    if c == 1 and on(1, i):
                        pe.wait_ge(*after("tn", i, 0))
                        pe.wait_ge(*free("gd_evac", i, (1, "router")))
                        for t in range(4):
                            for k in range(KT):
                                ins = mm(gd[:, t * NE:(t + 1) * NE], tn[:, k, t * P:(t + 1) * P], router_s[:, k, :],
                                         start=(k == 0), stop=(k == KT - 1))
                        ins.then_inc(sem["gd_full"], 1)
                    if c < 2 and on(2, i):
                        experts_down(c, range(8, 16), last=True)
                    if c == 1 and on(1, i):
                        pe.wait_ge(*after("topk", i, TOPK_STEPS - 1))
                        pe.wait_ge(*free("gd_evac", i, (1, "combT")))
                        for t in range(4):
                            ins = nc.tensor.transpose(gdt[:, t * P:(t + 1) * P], c24[:, t, :], ident_s[:])
                        ins.then_inc(sem["gd_full"], 1)
                    if c >= 2 and on(1, i):
                        if c == 2:
                            pe.wait_ge(*after("gd_evac", i, (1, "combT")))
                        experts_up(c)

            rounds(pe, one)

        @block.scalar
        def _(act):
            f = nc.scalar.activation
            act.preload_act_table_set("natural_log_exp_and_others")
            act.wait_ge(ready, READY)
            f(col("A", 0, UNITS), col("A_log", 0, UNITS), ACT.Exp).then_inc(setup_act, 1)
            act.wait_ge(setup_mm, 1)
            f(wdt_s[:], ga[:, 0:P], ACT.Copy).then_inc(setup_act, 1)
            f(col("bn_s", 0, KT), col("bn_var", 0, KT), ACT.Ln, bias=col("eps")).then_inc(setup_act, 1)
            act.wait_ge(setup_act, 3)
            f(col("bn_s", 0, KT), col("bn_s", 0, KT), ACT.Exp, scale=-0.5).then_inc(setup_act, 1)
            act.wait_ge(derived, 1)

            def one(i):
                for c in range(CH):
                    cn, par = (c + 1) % CH, (c + 1) % 2
                    for u in range(UNITS):
                        n = c * UNITS + u
                        if on(0, i):
                            act.wait_ge(*after("bcast", i, (c, u)))
                            f(a[:, n % 2, :], pa[n % 2][:], ACT.Exp, scale=col("A", group(u)[2])).then_inc(sem["exp"], 1)
                        if on(prep(c), i):
                            j = i + (1 if c == 3 else 0)
                            if u == 1:
                                act.wait_ge(*after("ga_full", i, (c, "X")))
                                act.wait_ge(*after("halo", i, (c - 1) % CH, back=1 if c == 0 else 0))
                                f(xh[:, KC - 1:], ga[:], ACT.Copy)
                                f(acc[:], ga[:], ACT.Identity, scale=col("conv", KC - 1), bias=col("b_conv"))
                                f(halo_at(j % PER_IMAGE, cn, 1), ga[:, T - KC + 1:T], ACT.Copy).then_inc(sem["ga_evac"], 1)
                                f(xh[:, 0:KC - 1], halo_at(j % PER_IMAGE, cn, 0), ACT.Copy).then_inc(sem["halo"], 1)
                            if u == 4:
                                act.wait_ge(*after("ga_full", i, (c, "Z")))
                                act.wait_ge(*after("zs", i, (c - 1) % CH, back=1 if c == 0 else 0))
                                f(zc[:], ga[:], ACT.Copy)
                                f(ez[:], ga[:], ACT.Exp, scale=-1.0).then_inc(sem["ga_evac"], 1)
                            if u == 5:
                                act.wait_ge(*after("conv", i, (c, KC - 2)))
                                f(ex[:], acc[:], ACT.Exp, scale=-1.0).then_inc(sem["neg_exp"], 1)
                            if u == 6:
                                act.wait_ge(*after("cap_z", i, c))
                                f(ez[:], ez[:], ACT.Ln, bias=col("one")).then_inc(sem["ln_z"], 1)
                            if u == 7:
                                act.wait_ge(*after("cap_x", i, c))
                                f(ex[:], ex[:], ACT.Ln, bias=col("one")).then_inc(sem["ln_x"], 1)
                                act.wait_ge(*after("ln_z", i, c))
                                f(ez[:], ez[:], ACT.Exp, scale=-1.0).then_inc(sem["gate_z"], 1)
                            if u == 8:
                                act.wait_ge(*after("ln_x", i, c))
                                f(ex[:], ex[:], ACT.Exp, scale=-1.0).then_inc(sem["gate_x"], 1)
                            if u == 11:
                                act.wait_ge(*after("ga_full", i, (c, "DT")))
                                act.wait_ge(*after("zs", i, c))
                                f(v[:], ga[:], ACT.Identity, bias=col("b_dt"))
                                f(ev[:], ga[:], ACT.Abs, bias=col("b_dt")).then_inc(sem["ga_evac"], 1)
                            if u == 12:
                                act.wait_ge(*after("ga_full", i, (c, "B")))
                                f(bs[:, par, :], ga[:], ACT.Copy).then_inc(sem["ga_evac"], 1)
                                act.wait_ge(*after("ga_evac", i, (c, "DT")))
                                f(ev[:], ev[:], ACT.Exp, scale=-1.0).then_inc(sem["sp_exp"], 1)
                            if u == 13:
                                act.wait_ge(*after("ga_full", i, (c, "C")))
                                f(cs[:, par, :], ga[:], ACT.Copy).then_inc(sem["ga_evac"], 1)
                                act.wait_ge(*after("sp_exp", i, c))
                                f(lnu[:], ev[:], ACT.Ln, bias=col("one")).then_inc(sem["sp_ln"], 1)
                        if c in (0, 2) and on(LATE[c], i):
                            if u == 6:
                                act.wait_ge(*after("ga_full", i, (c, "outp")))
                                f(yn[:], ga[:], ACT.Copy)
                                f(sq2[:, 0, :], ga[:], ACT.Square).then_inc(sem["ga_evac"], 1)
                            if u == 9:
                                act.wait_ge(*after("ga_full", i, (c, "var")))
                                f(rs2[:], ga[:], ACT.Ln, bias=col("eps")).then_inc(sem["ga_evac"], 1)
                            if u == 10:
                                act.wait_ge(*after("ga_evac", i, (c, "var")))
                                f(rs2[:], rs2[:], ACT.Exp, scale=-0.5).then_inc(sem["rstd"], 1)
                            if u == 14:
                                act.wait_ge(*after("yn", i, c))
                                f(yn[:], yn[:], ACT.Identity, scale=col("g1"), bias=col("b1")).then_inc(sem["yn_aff"], 1)
                        if c == 1 and on(1, i):
                            if u in (5, 7):
                                m = (u - 5) // 2
                                act.wait_ge(*after("ga_full", i, (c, f"wout{m}")))
                                f(oc[:, m, :], ga[:], ACT.Identity, scale=col("bn_s", m), bias=col("bn_t", m))
                                f(eo[:, m, :], ga[:], ACT.Exp, scale=col("bn_ns", m), bias=col("bn_nt", m)).then_inc(sem["ga_evac"], 1)
                            if u == 9:
                                act.wait_ge(*after("cap_o", i, 0))
                                f(eo, eo, ACT.Ln, bias=col("one")).then_inc(sem["ln_o"], 1)
                            if u == 10:
                                act.wait_ge(*after("ln_o", i, 0))
                                f(eo, eo, ACT.Exp, scale=-1.0).then_inc(sem["gate_o"], 1)
                            if u == 15:
                                act.wait_ge(*after("gd_evac", i, (1, "mean")))
                                f(sq2[:], tn[:], ACT.Square).then_inc(sem["tail_sq"], 1)
                        if c == 2 and u == 2:
                            if on(-1, i):
                                act.wait_ge(*after("gd_evac", i, (2, "hmean")))
                                f(sq2[:], xn[:], ACT.Square).then_inc(sem["head_sq"], 1)
                            if on(0, i):
                                act.wait_ge(*after("xs", i, 0, back=1))
                                for k in range(KT):
                                    f(skip[:, k, :], xs[:, k, :], ACT.Identity, scale=col("skip"), bias=col("b_fc2")).then_inc(sem["skip_in"], 1)
                        if c == 2 and u == 5 and on(-1, i):
                            act.wait_ge(*after("ga_full", i, (c, "hvar")))
                            f(rs2[:], ga[:], ACT.Ln, bias=col("head_add")).then_inc(sem["ga_evac"], 1)
                            act.wait_ge(*after("ga_evac", i, (c, "hvar")))
                            f(rs2[:], rs2[:], ACT.Exp, scale=-0.5).then_inc(sem["rstd_h"], 1)
                        if c == 2 and u == 8 and on(-1, i):
                            act.wait_ge(*after("xn", i, 0))
                            act.wait_ge(*after("ga_evac", i, (c, "Z")))
                            act.wait_ge(*after("skip_in", i, 1))
                            for k in range(KT):
                                ins = f(xs[:, k, :], xn[:, k, :], ACT.Identity, scale=col("g_head", k), bias=col("b", k))
                            ins.then_inc(sem["xs"], 1)
                    if on(prep(c), i):
                        act.wait_ge(*after("dt", i, c))
                        act.wait_ge(*after("dtx", i, c))
                        f(part[0][:], v2[:], ACT.Copy).then_inc(sem["hi"], 1)
                    if c == 1 and on(1, i):
                        act.wait_ge(*after("ga_full", i, (c, "tvar")))
                        f(rs2[:], ga[:], ACT.Ln, bias=col("eps")).then_inc(sem["ga_evac"], 1)
                        act.wait_ge(*after("ga_evac", i, (c, "tvar")))
                        f(rs2[:], rs2[:], ACT.Exp, scale=-0.5).then_inc(sem["rstd_t"], 1)
                    if on(prep(c), i):
                        act.wait_ge(*after("rest", i, c))
                        f(part[1][:], v2[:], ACT.Copy).then_inc(sem["mid"], 1)
                    if c in (0, 2) and on(LATE[c], i):
                        for hh in range(2):
                            for m in range(2):
                                act.wait_ge(*after("ga_full", i, (c, ("F", hh, m))))
                                f(gl[:, hh, m, :], ga[:], ACT.Gelu, bias=col("b_fc1", m)).then_inc(sem["ga_evac"], 1)
                    if c == 1 and on(1, i):
                        act.wait_ge(*after("topk", i, 8))
                        f(pr[:, 1, :], pr[:, 0, :], ACT.Exp).then_inc(sem["topk_exp"], 1)
                    if c >= 2 and on(1, i):
                        for e in range(4 * (c - 2), 4 * (c - 2) + 4):
                            act.wait_ge(*after("gh_full", i, e))
                            f(hc[:, e, 0, :], gh[:], ACT.Gelu, bias=col("moe_b1", 2 * e)).then_inc(sem["gh_evac"], 1)
                            act.wait_ge(*after("ga_full", i, (c, ("h", e))))
                            f(hc[:, e, 1, :], ga[:], ACT.Gelu, bias=col("moe_b1", 2 * e + 1)).then_inc(sem["ga_evac"], 1)
                    if c != 1:
                        act.preload_act_table_set("natural_log_exp_and_others")

            def halo_at(slot, cn, ahead):
                start = (slot + ahead) * (CH * (KC - 1)) + cn * (KC - 1)
                return halo[:, start:start + KC - 1] if isinstance(slot, int) else halo[:, bass.ds(start, KC - 1)]

            rounds(act, one)

        @block.vector
        def _(dve):
            tt, ts, stt = nc.vector.tensor_tensor, nc.vector.tensor_scalar, nc.vector.scalar_tensor_tensor
            nc.vector.memset(state[:], 0.0)
            nc.vector.memset(halo[:], 0.0)
            nc.vector.memset(wof_s[:], 0.0)
            nc.vector.memset(col("one"), 1.0)
            nc.vector.memset(col("eps"), LN_EPS)
            nc.vector.memset(col("head_add"), HEAD_ADD).then_inc(ready, 1)
            chain = [0]

            def link(ins):
                chain[0] += 1
                ins.then_inc(setup_dve, 1)
                dve.wait_ge(setup_dve, chain[0])

            dve.wait_ge(ready, READY)
            dve.wait_ge(setup_act, 4)
            link(ts(col("A", 0, UNITS), col("A", 0, UNITS), -1.0, None, ALU.mult))
            link(ts(col("g_head", 0, KT), col("g", 0, KT), HEAD_SCALE, None, ALU.mult))
            link(ts(col("bn_v", 0, KT), col("bn_var", 0, KT), LN_EPS, -0.5, ALU.add, ALU.mult))
            link(tt(col("bn_v", 0, KT), col("bn_v", 0, KT), col("bn_s", 0, KT), ALU.mult))
            link(tt(col("bn_v", 0, KT), col("bn_v", 0, KT), col("bn_s", 0, KT), ALU.mult))
            link(ts(col("bn_v", 0, KT), col("bn_v", 0, KT), 1.5, None, ALU.add))
            link(tt(col("bn_s", 0, KT), col("bn_s", 0, KT), col("bn_v", 0, KT), ALU.mult))
            link(tt(col("bn_s", 0, KT), col("bn_s", 0, KT), col("bn_g", 0, KT), ALU.mult))
            link(tt(col("bn_t", 0, KT), col("bn_s", 0, KT), col("bn_mean", 0, KT), ALU.mult))
            link(tt(col("bn_t", 0, KT), col("bn_b", 0, KT), col("bn_t", 0, KT), ALU.subtract))
            link(ts(col("bn_ns", 0, KT), col("bn_s", 0, KT), -1.0, None, ALU.mult))
            link(ts(col("bn_nt", 0, KT), col("bn_t", 0, KT), -1.0, None, ALU.mult))
            link(nc.vector.reduce_sum(wo_mean[:], wo_s[:], axis=AX_X))
            link(ts(wo_mean[:], wo_mean[:], 1.0 / DM, None, ALU.mult))
            for k in range(2):
                link(ts(wof_s[:, k, k * DM:(k + 1) * DM], wo_s[:], wo_mean[:, 0:1], None, ALU.subtract))
            dve.sem_inc(derived, 1)

            def state_at(slot, n):
                start = slot * (CH * UNITS) + n
                return state[:, start:start + 1] if isinstance(slot, int) else state[:, bass.ds(start, 1)]

            def one(i):
                for c in range(CH):
                    cn, par = (c + 1) % CH, (c + 1) % 2
                    was = (c - 1) % CH
                    for u in range(UNITS):
                        n = c * UNITS + u
                        if on(0, i):
                            dve.wait_ge(*after("bcast", i, (c, u)))
                            if u == 0:
                                dve.wait_ge(*after("ga_evac", i, (was, "C"), back=1 if c == 0 else 0))
                            tt(pb[n % 2][:], pb[n % 2][:], bs[:, c % 2, :], ALU.mult).then_inc(sem["bx"], 1)
                            dve.wait_ge(*after("exp", i, (c, u)))
                            dve.wait_ge(*after("bx", i, (c, u)))
                            nc.vector.tensor_tensor_scan(h[:, n % RING, :], a[:, n % 2, :], pb[n % 2][:], state_at(i % PER_IMAGE, n),
                                                         ALU.mult, ALU.add).then_inc(sem["scan"], 1)
                        if on(prep(c), i):
                            if u in (2, 3, 4):
                                k = u - 2
                                if k == 0:
                                    dve.wait_ge(*after("halo", i, c))
                                else:
                                    dve.wait_ge(*after("conv", i, (c, k - 1)))
                                stt(acc[:], xh[:, k:k + T], col("conv", k), acc[:], ALU.mult, ALU.add).then_inc(sem["conv"], 1)
                            if u == 5:
                                dve.wait_ge(*after("ga_evac", i, (c, "Z")))
                                ts(ez[:], ez[:], EXP_CAP, None, ALU.min).then_inc(sem["cap_z"], 1)
                            if u == 6:
                                dve.wait_ge(*after("neg_exp", i, c))
                                ts(ex[:], ex[:], EXP_CAP, None, ALU.min).then_inc(sem["cap_x"], 1)
                            if u == 9:
                                dve.wait_ge(*after("gate_x", i, c))
                                tt(xcs[:, par, :], acc[:], ex[:], ALU.mult).then_inc(sem["xc"], 1)
                            if u == 11:
                                dve.wait_ge(*after("ga_evac", i, (c, "DT")))
                                ts(v[:], v[:], 0.0, None, ALU.max).then_inc(sem["sp_max"], 1)
                            if u == 13:
                                dve.wait_ge(*after("sp_exp", i, c))
                                ts(dr[:], ev[:], 1.0, 1.0, ALU.add, ALU.subtract).then_inc(sem["sp_round"], 1)
                            if u == 14:
                                dve.wait_ge(*after("sp_ln", i, c))
                                dve.wait_ge(*after("sp_err", i, c))
                                tt(lnu[:], lnu[:], dr[:], ALU.add).then_inc(sem["sp_sum"], 1)
                            if u == 15:
                                dve.wait_ge(*after("sp_sum", i, c))
                                dve.wait_ge(*after("sp_max", i, c))
                                tt(v2[:, 0, :], lnu[:], v[:], ALU.add).then_inc(sem["dt"], 1)
                        if u == 3 and on(prev(c), i):
                            dve.wait_ge(*after("yred", i, (c, "prev")))
                            stt(yg[:, was % 2, :], xcs[:, was % 2, :], col("D"), py[:], ALU.mult, ALU.add).then_inc(sem["yd"], 1)
                        if c in (1, 3) and u == 2 and on(LATE[c], i):
                            pair = 1 if c == 1 else 0
                            dve.wait_ge(*after("gd_full", i, (c, "fc2")))
                            dve.wait_ge(*after("skip_in", i, 1, back=1 if c == 1 else 0))
                            tt(skip[:, pair, :], skip[:, pair, :], gd[:], ALU.add).then_inc(sem["gd_evac"], 1)
                        if c == 1 and on(1, i):
                            if u == 8:
                                dve.wait_ge(*after("ga_evac", i, (1, "wout1")))
                                ts(eo, eo, EXP_CAP, None, ALU.min).then_inc(sem["cap_o"], 1)
                            if u == 11:
                                dve.wait_ge(*after("gate_o", i, 0))
                                tt(oc, oc, eo, ALU.mult).then_inc(sem["o"], 1)
                            if u == 14:
                                dve.wait_ge(*after("gd_full", i, (1, "mean")))
                                dve.wait_ge(*after("fin", i, 0, back=1))
                                for m in range(KT):
                                    ins = tt(tn[:, m, :], x1[:, m, :], gd[:], ALU.subtract)
                                ins.then_inc(sem["gd_evac"], 1)
                        if c == 2 and on(-1, i):
                            if u == 1:
                                dve.wait_ge(*after("gd_full", i, (2, "hmean")))
                                for m in range(KT):
                                    ins = tt(xn[:, m, :], xn[:, m, :], gd[:], ALU.subtract)
                                ins.then_inc(sem["gd_evac"], 1)
                            if u == 7:
                                dve.wait_ge(*after("rstd_h", i, 0))
                                for m in range(KT):
                                    ins = tt(xn[:, m, :], xn[:, m, :], rs2[:], ALU.mult)
                                ins.then_inc(sem["xn"], 1)
                    if on(prep(c), i):
                        dve.wait_ge(*after("hi", i, c))
                        tt(v2[:], v2[:], part[0][:], ALU.subtract).then_inc(sem["rest"], 1)
                        dve.wait_ge(*after("mid", i, c))
                        tt(part[2][:], v2[:], part[1][:], ALU.subtract).then_inc(sem["lo"], 1)
                    if c == 1 and on(1, i):
                        dve.wait_ge(*after("rstd_t", i, 0))
                        for m in range(KT):
                            ins = tt(tn[:, m, :], tn[:, m, :], rs2[:], ALU.mult)
                        ins.then_inc(sem["tn"], 1)
                        topk(i)
                    if c < 2 and on(2, i):
                        dve.wait_ge(*after("moe_full", i, c))
                        if c == 0:
                            dve.wait_ge(*after("fin", i, 0, back=1))
                        tt(fin[:, c, :], fin[:, c, :], gh[:], ALU.add).then_inc(sem["moe_evac"], 1)
                    if c == 1 and on(1, i):
                        dve.wait_ge(*after("gd_full", i, (1, "combT")))
                        nc.vector.tensor_copy(combT[:], gdt)
                        nc.vector.tensor_copy(combTf[:], gdt).then_inc(sem["gd_evac"], 1)
                    if c >= 2 and on(1, i):
                        for e in range(4 * (c - 2), 4 * (c - 2) + 4):
                            dve.wait_ge(*after("gd_full", i, (c, ("bc", e))))
                            dve.wait_ge(*after("ga_evac", i, (c, ("h", e))))
                            dve.wait_ge(*after("gh_evac", i, e))
                            for m in range(2):
                                ins = tt(hc[:, e, m, :], hc[:, e, m, :], gd[:], ALU.mult)
                            ins.then_inc(sem["gd_evac"], 1)

            def topk(i):
                step = [0]

                def mark(ins):
                    ins.then_inc(sem["topk"], 1)
                    step[0] += 1

                def then(ins):
                    mark(ins)
                    dve.wait_ge(*after("topk", i, step[0] - 1))

                dve.wait_ge(*after("gd_full", i, (1, "router")))
                nc.vector.tensor_copy(lg[:], gd[:, 0:4 * NE].rearrange("p (t e) -> p t e", e=NE)).then_inc(sem["gd_evac"], 1)
                dve.wait_ge(*after("gd_evac", i, (1, "router")))
                dve.sem_inc(gate, 1)
                for t in range(4):
                    mark(nc.vector.max(mx[:, t, :], lg[:, t, :]))
                dve.wait_ge(*after("topk", i, 3))
                dve.sem_inc(gate, 1)
                for t in range(4):
                    mark(nc.vector.max_index(ix[:, t, :], mx[:, t, :], lg[:, t, :]))
                mark(tt(pr[:, 0, :], mx[:, :, 1], mx[:, :, 0], ALU.subtract))
                dve.wait_ge(*after("topk", i, 7))
                then(nc.vector.tensor_copy(ixf[:], ix[:, :, 0:2]))
                for k in range(2):
                    mark(tt(cmp[:, k, :, :], iota_s[:], ixf[:, :, k:k + 1].to_broadcast([P, 4, NE]), ALU.is_equal))
                dve.wait_ge(*after("topk_exp", i, 0))
                then(ts(pr[:, 2, :], pr[:, 1, :], 1.0, None, ALU.add))
                then(nc.vector.reciprocal(pr[:, 2, :], pr[:, 2, :]))
                then(tt(pr[:, 3, :], pr[:, 2, :], pr[:, 1, :], ALU.mult))
                mark(tt(cmp[:, 0, :, :], cmp[:, 0, :, :], pr[:, 2, :].unsqueeze(2).to_broadcast([P, 4, NE]), ALU.mult))
                then(tt(cmp[:, 1, :, :], cmp[:, 1, :, :], pr[:, 3, :].unsqueeze(2).to_broadcast([P, 4, NE]), ALU.mult))
                then(tt(comb[:], cmp[:, 0, :, :], cmp[:, 1, :, :], ALU.add))
                then(nc.vector.tensor_copy(c24[:, :, 0:NE], comb[:]))
                then(tt(comb[:], comb[:], c24[:, :, 0:NE], ALU.subtract))
                then(nc.vector.tensor_copy(c24[:, :, NE:2 * NE], comb[:]))
                mark(tt(c24[:, :, 2 * NE:3 * NE], comb[:], c24[:, :, NE:2 * NE], ALU.subtract))
                assert step[0] == TOPK_STEPS

            rounds(dve, one)

        @block.gpsimd
        def _(pool):
            tt = nc.gpsimd.tensor_tensor
            pool.wait_ge(derived, 1)

            def state_at(slot, n):
                start = (slot + 1) * (CH * UNITS) + n
                return state[:, start:start + 1] if isinstance(slot, int) else state[:, bass.ds(start, 1)]

            def one(i):
                for c in range(CH):
                    cn, par = (c + 1) % CH, (c + 1) % 2
                    was = (c - 1) % CH
                    for u in range(UNITS):
                        n = c * UNITS + u
                        if on(0, i):
                            pool.wait_ge(*after("scan", i, (c, u)))
                            nc.gpsimd.tensor_copy(state_at(i % PER_IMAGE, n), h[:, n % RING, T - 1:T]).then_inc(sem["saved"], 1)
                            pool.wait_ge(*after("saved", i, (c, u)))
                            tt(h[:, n % RING, :], h[:, n % RING, :], cs[:, c % 2, :], ALU.mult).then_inc(sem["prod"], 1)
                        if u == 3 and on(prev(c), i):
                            pool.wait_ge(*after("yd", i, c))
                            tt(yg[:, was % 2, :], yg[:, was % 2, :], zs[:, was % 2, :], ALU.mult).then_inc(sem["yg"], 1)
                        if on(prep(c), i):
                            if u == 8:
                                pool.wait_ge(*after("gate_z", i, c))
                                tt(zs[:, par, :], zc[:], ez[:], ALU.mult).then_inc(sem["zs"], 1)
                            if u == 13:
                                pool.wait_ge(*after("sp_round", i, c))
                                tt(dr[:], ev[:], dr[:], ALU.subtract).then_inc(sem["sp_err"], 1)
                            if u == 15:
                                pool.wait_ge(*after("dt", i, c))
                                tt(v2[:, 1, :], v2[:, 0, :], xcs[:, par, :], ALU.mult).then_inc(sem["dtx"], 1)
                        if c in (0, 2) and u == 10 and on(LATE[c], i):
                            pool.wait_ge(*after("rstd", i, c))
                            tt(yn[:], yn[:], rs2[:], ALU.mult).then_inc(sem["yn"], 1)
                        if c == 1 and on(1, i) and u == 11:
                            pool.wait_ge(*after("o", i, 0))
                            pool.wait_ge(*after("xr", i, 0))
                            tt(x1[:], x1[:], oc, ALU.add).then_inc(sem["x1"], 1)
                    if c == 1 and on(1, i):
                        pool.wait_ge(*after("tn", i, 0))
                        pool.wait_ge(*after("stored", i, 1))
                        tt(fin[:], x1[:], tn[:], ALU.add).then_inc(sem["fin"], 1)

            rounds(pool, one)


def kernel(**inputs):
    import ml_dtypes
    import numpy as np
    import concourse.bacc as bacc
    from concourse.bass_utils import run_bass_kernel_spmd

    g = {k: np.asarray(v) for k, v in inputs.items()}
    L0 = {k[len("L0_conv_"):]: v for k, v in g.items() if k.startswith("L0_conv_")}
    FF = {k[len("L0_ffn_"):]: v for k, v in g.items() if k.startswith("L0_ffn_")}
    f32, bf = np.float32, ml_dtypes.bfloat16

    def halves(v):
        return v.reshape(KT, P).T

    def twice(v):
        return np.concatenate([v, v])[:, None]

    small = np.concatenate([
        L0["W_conv"].reshape(DI, KC), L0["b_conv"][:, None], L0["b_dt"][:, None], L0["D_par"][:, None],
        halves(L0["g_norm"]), halves(L0["b_norm"]), twice(L0["g_norm1"]), twice(L0["b_norm1"]),
        L0["b_fc1"].reshape(2, P).T, twice(L0["b_fc2"]), np.broadcast_to(L0["skip_scale"], (P, 1)),
        halves(L0["bn_g"]), halves(L0["bn_b"]), halves(L0["bn_mean"]), halves(L0["bn_var"]),
        FF["b1"].reshape(NE, 2, P).transpose(2, 0, 1).reshape(P, 2 * NE),
        L0["A_log"].reshape(UNITS, P).T], 1)

    def at_half(w):
        o = np.zeros((P, 2, w.shape[1]), w.dtype)
        for k in range(2):
            o[k * DM:(k + 1) * DM, k] = w
        return o

    W_in, Wx = L0["W_in"], L0["W_xproj"]
    wf2 = np.zeros((P, 2, 2, P), f32)
    for k in range(2):
        for h in range(2):
            wf2[:, k, h, h * DM:(h + 1) * DM] = L0["W_fc2"].T[k * P:(k + 1) * P]
    wout = L0["W_out"].T.reshape(DM, CH, C).transpose(1, 0, 2).reshape(KT, P, C).transpose(1, 0, 2)
    experts = lambda w: w.reshape(NE, KT, P, C).transpose(2, 0, 1, 3)
    p = np.arange(P)
    red = np.zeros((P, 4, 32), f32)
    sel = np.zeros((PARTS, 32, 4, P), f32)
    for r in range(4):
        red[p, r, 8 * r + p // NS] = 1
        sel[:, 8 * r + p // NS, r, p] = 1
    sele = np.zeros((PARTS, NE, NE, P), f32)
    for e in range(NE):
        sele[:, e, e, :] = 1
    arrays = dict(
        x=g["x"].reshape(B, KT, P, PER_IMAGE, T).transpose(0, 3, 2, 1, 4).reshape(TILES, P, KT, T),
        small=small, wx=at_half(W_in[:DI].T), wz=at_half(W_in[DI:].T), wdtl=Wx[:RK], wdtr=L0["W_dt"].T,
        wb=Wx[RK:RK + NS].T[:, p % NS], wc=Wx[RK + NS:].T[:, p % NS], wo=L0["W_outp"].T,
        wf1=at_half(L0["W_fc1"].T), wf2=wf2, wout=wout, w1=experts(FF["w1"]), w2=experts(FF["w2"]),
        b2=np.concatenate([FF["b2"]] * PARTS), router=FF["router_w"].T.reshape(KT, P, NE).transpose(1, 0, 2),
        mean256=np.full((P, P), 1 / C, f32), mean64=np.kron(np.eye(2), np.full((DM, DM), 1 / DM)).astype(f32),
        red=red, iota=np.broadcast_to(np.arange(NE, dtype=f32), (P, 4, NE)),
        sel=sel.reshape(PARTS * 32, 4, P).astype(bf), sele=sele.reshape(PARTS * NE, NE, P).astype(bf),
        ident=np.eye(P, dtype=f32).astype(bf))
    arrays = {k: np.ascontiguousarray(v) for k, v in arrays.items()}

    nc = bacc.Bacc("TRN2", target_bir_lowering=False, num_devices=1)
    args = {k: nc.dram_tensor(f"in_{k}", v.shape, mybir.dt.from_np(v.dtype), kind="ExternalInput").ap() for k, v in arrays.items()}
    out = nc.dram_tensor("out_y", (TILES, P, KT, T), F32, kind="ExternalOutput").ap()
    build(nc, **args, out=out)
    r = run_bass_kernel_spmd(nc, [{f"in_{k}": v for k, v in arrays.items()}], core_ids=[0])
    y = np.asarray(r.results[0]["out_y"])
    return y.reshape(B, PER_IMAGE, P, KT, T).transpose(0, 3, 2, 1, 4).reshape(B, C, H, W)
```

```python
from contextlib import ExitStack

import concourse.bass as bass
from concourse import mybir

F32 = mybir.dt.float32
BF16 = mybir.dt.bfloat16
U32 = mybir.dt.uint32
ALU = mybir.AluOpType
ACT = mybir.ActivationFunctionType
AX_X = mybir.AxisListType.X

P = 128
B, C, H, W = 4, 256, 64, 64
L = H * W
T = 512
KT = C // P
TILES = B * L // T
PER_IMAGE = L // T
CH = 4
DM = C // CH
DI = 2 * DM
NS = 16
KC = 4
RK = 4
UNITS = DI * NS // P
JU = P // NS
NE = 8
PARTS = 3
RING = 8
DOWN_SLOTS = [0, 1, 2, 3, 4, 5, 10, 12, 13, 15]
TOPK_STEPS = 22
LN_EPS = 1e-5
LNC_EPS = 1e-6
HEAD_ADD = LNC_EPS * LN_EPS / (1.0 + LN_EPS)
HEAD_SCALE = (1.0 + LN_EPS) ** -0.5
EXP_CAP = 2.0 ** 60

SMALL = dict(conv=KC, b_conv=1, b_dt=1, D=1, g=KT, b=KT, g1=1, b1=1, b_fc1=2, b_fc2=1, skip=1,
             bn_g=KT, bn_b=KT, bn_mean=KT, bn_var=KT, moe_b1=NE * 2, A_log=UNITS,
             A=UNITS, g_head=KT, bn_s=KT, bn_t=KT, bn_ns=KT, bn_nt=KT, bn_v=KT, one=1, eps=1, head_add=1)
LOADED = sum(list(SMALL.values())[:17])
COL, _at = {}, 0
for _name, _n in SMALL.items():
    COL[_name] = _at
    _at += _n
NSMALL = _at

def prep(c):
    return -1 if c == CH - 1 else 0


def prep_in(c):
    return -1 if c >= CH - 2 else 0


LATE = {0: 1, 1: 1, 2: 0, 3: 0}
_prep = [(c, prep(c)) for c in range(CH)]
_prep_in = [(c, prep_in(c)) for c in range(CH)]
_chunk = [(c, 0) for c in range(CH)]
_unit = [((c, u), 0) for c in range(CH) for u in range(UNITS)]
_pairs = [(0, 1), (2, 0)]
_fc1 = [("F", h, m) for h in range(2) for m in range(2)]
_up = {c: [("h", e, m) for e in range(4 * (c - 2), 4 * (c - 2) + 4) for m in range(2)] for c in (2, 3)}
GA_ORDER = {0: ["DT", "B", "C", "outp", "var", "X"] + _fc1 + ["Z"],
            1: ["wout0", "wout1", "DT", "B", "C", "tvar", "X", "Z", "router", "combT"],
            2: ["hvar", "DT", "B", "C", "outp", "var", "X"] + _fc1 + ["Z"] + _up[2],
            3: ["DT", "B", "C", "X", "Z"] + _up[3]}


def _ga_lag(c, n):
    if n in ("DT", "B", "C"):
        return prep(c)
    if n in ("X", "Z"):
        return prep_in(c)
    if n == "hvar":
        return -1
    if n in ("wout0", "wout1", "tvar", "router", "combT") or n[0] == "h":
        return 1
    return LATE[c]


_ga = [((c, n), _ga_lag(c, n)) for c in range(CH) for n in GA_ORDER[c]]
_gd = [((0, "down"), 2), ((1, "fc2"), 1), ((1, "mean"), 1), ((1, "down"), 2), ((2, "hmean"), -1)] \
    + [((2, ("bc", e)), 1) for e in range(4)] + [((3, "fc2"), 0)] + [((3, ("bc", e)), 1) for e in range(4, 8)]
EVENTS = dict(
    bcast_a=_unit, bcast_b=_unit, yred=_chunk, ga_full=_ga, gd_full=_gd,
    ga_evac=_ga, exp=_unit, halo=_prep_in, neg_exp=_prep, ln_g=_prep, gate=_prep,
    ln_o=[(0, 1)], gate_o=[(0, 1)], rstd=_pairs, rstd_h=[(0, -1)], rstd_t=[(0, 1)], sp_exp=_prep, sp_ln=_prep,
    hi=_prep, mid=_prep, yn_aff=_pairs, skip_in=[(0, 0), (1, 0)], tail_sq=[(0, 1)], head_sq=[(0, -1)],
    xs=[(0, -1)], topk_exp=[(0, 1)],
    gd_evac=_gd, bx=_unit, scan=_unit, conv=[((c, k), lag) for c, lag in _prep_in for k in range(KC - 1)],
    yd=_chunk, cap=_prep, cap_o=[(0, 1)], sp_max=_prep, sp_round=_prep, xc=_prep, sp_sum=_prep, dt=_prep,
    rest=_prep, lo=_prep, o=[(0, 1)], tn=[(0, 1)], xn=[(0, -1)], topk=[(k, 1) for k in range(TOPK_STEPS)],
    saved=_unit, prod=_unit, yg=_chunk, zs=_prep, sp_err=_prep, dtx=_prep, yn=_pairs, x1=[(0, 1)], fin=[(0, 1)],
    xt=[(0, -1)], xr=[(0, 1)], stored=[(0, 2), (1, 2)],
    shuffle0=[((c, k), lag) for c, lag in _prep if c % 2 == 1 for k in range(PARTS * 4)],
    shuffle1=[((c, k), lag) for c, lag in _prep if c % 2 == 0 for k in range(PARTS * 4)],
)
DMA_COUNTED = ("xt", "xr", "stored", "shuffle0", "shuffle1")
FIRST, LAST = -1, TILES + 1
LOOP = (3, TILES - 1)


def on(lag, i):
    return not isinstance(i, int) or 0 <= i - lag < TILES


def _in_round(name, i):
    return [k for k, lag in EVENTS[name] if on(lag, i)]


def _before(name, i):
    return sum(len(_in_round(name, j)) for j in range(FIRST, i))


def count(name, i, key=None, back=0):
    n = len(EVENTS[name])
    unit = 16 if name in DMA_COUNTED else 1
    if isinstance(i, int):
        keys = _in_round(name, i - back)
        if key is None:
            return _before(name, i) * unit
        return (_before(name, i - back) + keys.index(key) + 1) * unit if key in keys else 0
    lags = {lag for _, lag in EVENTS[name]}
    assert not back or 2 not in lags or lags == {2}
    index = 0 if key is None else [k for k, _ in EVENTS[name]].index(key) + 1
    constant = _before(name, LOOP[0]) + index - n * back - n * LOOP[0]
    assert n * LOOP[0] + constant > 0
    return i * (n * unit) + constant * unit


GA_KEYS = [k for k, _ in _ga]
assert len(GA_KEYS) % 2 == 0


def ga_bank(key):
    return GA_KEYS.index(key) % 2


def ga_before(i, key):
    at = GA_KEYS.index(key)
    if not isinstance(i, int):
        return count("ga_evac", i, GA_KEYS[at - 2]) if at >= 2 else count("ga_evac", i) - (1 - at)
    for j in range(i, FIRST - 1, -1):
        for k in range(at - 2 if j == i else len(GA_KEYS) - 2 + at % 2, -1, -2):
            if GA_KEYS[k] in _in_round("ga_evac", j):
                return _before("ga_evac", j) + _in_round("ga_evac", j).index(GA_KEYS[k]) + 1
    return 0


def build(nc, x, small, wx, wz, wdtl, wdtr, wb, wc, wo, wf1, wf2, wout, w1, w2, b2, router,
          mean256, mean64, red, iota, sel, sele, ident, out):
    with ExitStack() as ctx:
        def sb(name, shape, dt=F32):
            return ctx.enter_context(nc.sbuf_tensor(name, shape, dt))

        def bank(name):
            return ctx.enter_context(nc.psum_tensor(name, [P, T], F32))

        sem = {name: ctx.enter_context(nc.semaphore(name)) for name in EVENTS}
        ready = ctx.enter_context(nc.semaphore("ready"))
        derived = ctx.enter_context(nc.semaphore("derived"))
        unheeded = ctx.enter_context(nc.semaphore("unheeded"))
        setup_mm = ctx.enter_context(nc.semaphore("setup_mm"))
        setup_act = ctx.enter_context(nc.semaphore("setup_act"))
        setup_dve = ctx.enter_context(nc.semaphore("setup_dve"))

        small_s = sb("small_s", [P, NSMALL])
        wx_s, wz_s = sb("wx_s", [P, 2, P]), sb("wz_s", [P, 2, P])
        wdtl_s, wdtr_s, wdt_s = sb("wdtl_s", [RK, P]), sb("wdtr_s", [RK, P]), sb("wdt_s", [P, P])
        wb_s, wc_s = sb("wb_s", [P, P]), sb("wc_s", [P, P])
        wo_s = sb("wo_s", [P, DM])
        wf1_s, wf2_s = sb("wf1_s", [P, 2, C]), sb("wf2_s", [P, 2, DM])
        wout_s = sb("wout_s", [P, KT, C])
        w1_s, w2_s = sb("w1_s", [P, NE, KT, C]), sb("w2_s", [P, NE, KT, C])
        b2_s, router_s = sb("b2_s", [PARTS * NE, C]), sb("router_s", [P, KT, NE])
        mean256_s, mean64_s = sb("mean256_s", [P, P]), sb("mean64_s", [P, P])
        red_s, iota_s = sb("red_s", [P, 4, 32]), sb("iota_s", [P, 4, NE])
        sel_s = sb("sel_s", [PARTS * 32, 4, P], BF16)
        sele_s, ident_s = sb("sele_s", [PARTS * NE, NE, P], BF16), sb("ident_s", [P, P], BF16)
        wo_mean = sb("wo_mean", [P, 1])

        def col(name, k=0, n=1):
            return small_s[:, COL[name] + k:COL[name] + k + n]

        state = sb("state", [P, (PER_IMAGE + 1) * CH * UNITS])
        halo = sb("halo", [P, (PER_IMAGE + 1) * CH * (KC - 1)])

        xn, xs = sb("xn_s", [P, KT, T]), sb("xs_s", [P, KT, T])
        sq2, rs2 = sb("sq2", [P, KT, T]), sb("rs2", [P, T])
        xh = sb("xh", [P, T + KC - 1])
        za, ge = sb("za", [P, 2, T]), sb("ge", [P, 2, T])
        zc, acc = za[:, 0, :], za[:, 1, :]
        v, dr, ev, lnu = za[:, 0, :], za[:, 1, :], ge[:, 0, :], ge[:, 1, :]
        xcs, zs = sb("xcs", [P, 2, T]), sb("zs_s", [P, 2, T])
        bs, cs = sb("bs", [P, 2, T]), sb("cs", [P, 2, T])
        v2 = sb("v2", [P, 2, T])
        part = [sb(n, [P, 2, T], BF16) for n in ("hi_s", "mid_s", "lo_s")]
        pd = [sb(f"pd{k}", [PARTS * 32, 2, 4, T], BF16) for k in range(2)]
        bx = sb("bx_s", [P, 3, T])
        h = sb("h", [P, RING, T])
        yg = sb("yg_s", [P, 2, T])
        yn, gl = sb("yn_s", [P, T]), sb("gl", [P, 2, 2, T])
        skip = sb("skip_s", [P, KT, T])
        oc, eo = gl[:, 0, :, :], gl[:, 1, :, :]
        x1, tn, fin = (sb(n, [P, KT, T]) for n in ("x1_s", "tn_s", "fin_s"))
        hc = sb("hc", [P, NE, 2, T])
        lg, mx, comb, cmp = sb("lg", [P, 4, NE]), sb("mx", [P, 4, 8]), sb("comb", [P, 4, NE]), sb("cmp", [P, 2, 4, NE])
        ix, ixf, pr = sb("ix", [P, 4, 8], U32), sb("ixf", [P, 4, 2]), sb("pr", [P, 4, 4])
        c24 = sb("c24", [P, 4, PARTS * NE], BF16)
        combT, combTf = sb("combT", [PARTS * NE, T], BF16), sb("combTf", [PARTS * NE, T])

        pa, pb = [bank(f"pa{k}") for k in range(2)], [bank(f"pb{k}") for k in range(2)]
        py, ga2, gd = bank("py"), [bank(f"ga{k}") for k in range(2)], bank("gd")

        loads = [(small_s[:, 0:LOADED], small), (wx_s, wx), (wz_s, wz), (wdtl_s, wdtl), (wdtr_s, wdtr),
                 (wb_s, wb), (wc_s, wc), (wo_s, wo), (wf1_s, wf1), (wf2_s, wf2), (wout_s, wout), (w1_s, w1),
                 (w2_s, w2), (b2_s, b2), (router_s, router), (mean256_s, mean256), (mean64_s, mean64),
                 (red_s, red), (iota_s, iota), (sel_s, sel), (sele_s, sele), (ident_s, ident)]
        READY = 16 * len(loads) + 1

        def met(name, n):
            return (sem[name], n) if not isinstance(n, int) or n > 0 else (derived, 1)

        def after(name, i, key, back=0):
            return met(name, count(name, i, key, back))

        def gd_free(i, key):
            return met("gd_evac", count("gd_evac", i, key) - 1)

        def ga_free(i, key):
            return met("ga_evac", ga_before(i, key))

        def rounds(eng, one):
            for i in range(FIRST, LOOP[0]):
                one(i)
            with eng.Fori(*LOOP) as i:
                one(i)
            for i in range(LOOP[1], LAST + 1):
                one(i)

        def group(u):
            q, r = u % 4, u // 4
            return q, r, 4 * q + r

        def transposed(bank_):
            return bank_[0:PARTS * NE, 0:T // 2].bitcast(BF16)

        block = ctx.enter_context(nc.Block())

        @block.sync
        def _(sp):
            for dst, src in loads:
                sp.dma_start(dst if isinstance(dst, bass.AP) else dst[:], src).then_inc(ready, 16)

            def one(i):
                if on(1, i):
                    sp.wait_ge(*after("fin", i, 0, back=1))
                    sp.dma_start(x1[:], tile(x, i - 1)).then_inc(sem["xr"], 16)
                if on(-1, i):
                    sp.wait_ge(*after("xs", i, 0, back=1))
                    sp.dma_start(xn[:], tile(x, i + 1)).then_inc(sem["xt"], 16)
                for c in range(CH):
                    if on(prep(c), i):
                        cn = (c + 1) % CH
                        for k, what in enumerate(("hi", "mid", "lo")):
                            sp.wait_ge(*after(what, i, c))
                            for q in range(4):
                                sp.dma_start(pd[cn % 2][32 * k:32 * k + 32, :, q, :],
                                             part[k][32 * q:32 * q + 32, :, :]).then_inc(sem[f"shuffle{cn % 2}"], 16)
                    if c < 2 and on(2, i):
                        sp.wait_ge(*after("gd_evac", i, (c, "down")))
                        sp.dma_start(tile(out, i - 2)[:, c, :], fin[:, c, :]).then_inc(sem["stored"], 16)

            def tile(dram, j):
                return dram[j] if isinstance(j, int) else dram[bass.ds(j, 1)].rearrange("a p k t -> (a p) k t")

            rounds(sp, one)
            sp.wait_ge(sem["stored"], 16 * KT * TILES)

        @block.tensor
        def _(pe):
            mm = nc.tensor.matmul
            pe.wait_ge(ready, READY)
            mm(gd[:, 0:P], wdtl_s[:], wdtr_s[:], start=True, stop=True).then_inc(setup_mm, 1)
            pe.wait_ge(derived, 1)

            def one(i):
                def bcast(c, u):
                    q, r, _ = group(u)
                    n = c * UNITS + u
                    if u == 0:
                        pe.wait_ge(*after(f"shuffle{c % 2}", i, ((c - 1) % CH, PARTS * 4 - 1), back=1 if c == 0 else 0))
                    was, back = ((n - 2) // UNITS, 0) if n >= 2 else (CH - 1, 1)
                    pe.wait_ge(*after("bx", i, (was, (n - 2) % UNITS), back=back))
                    mm(pb[n % 2][:], sel_s[:, r, :], pd[c % 2][:, 1, q, :], start=True, stop=True).then_inc(sem["bcast_b"], 1)
                    pe.wait_ge(*after("scan", i, (was, (n - 2) % UNITS), back=back))
                    mm(pa[n % 2][:], sel_s[:, r, :], pd[c % 2][:, 0, q, :], start=True, stop=True).then_inc(sem["bcast_a"], 1)

                def reduce(c, k):
                    pe.wait_ge(*after("prod", i, (c, 4 * k + 3)))
                    if k == 0:
                        pe.wait_ge(*after("yd", i, (c - 1) % CH, back=1 if c == 0 else 0))
                    for q in range(4):
                        n = c * UNITS + 4 * k + q
                        ins = mm(py[32 * q:32 * q + 32, :], red_s[:, k, :], h[:, n % RING, :], start=(k == 0), stop=(k == 3))
                    if k == 3:
                        ins.then_inc(sem["yred"], 1)

                def to_act(c, name, pieces):
                    bank_ = ga2[ga_bank((c, name))]
                    pe.wait_ge(*ga_free(i, (c, name)))
                    for k, (w, r) in enumerate(pieces):
                        ins = mm(bank_[:], w, r, start=(k == 0), stop=(k == len(pieces) - 1))
                    ins.then_inc(sem["ga_full"], 1)

                def to_dve(c, name, pieces):
                    pe.wait_ge(*gd_free(i, (c, name)))
                    for k, (w, r) in enumerate(pieces):
                        ins = mm(gd[:], w, r, start=(k == 0), stop=(k == len(pieces) - 1))
                    ins.then_inc(sem["gd_full"], 1)

                def down(m, n):
                    if n < 0:
                        pe.wait_ge(*gd_free(i, (m, "down")))
                        mm(gd[:], b2_s[:, m * P:m * P + P], combTf[:], start=True, stop=False)
                        return
                    e, k = divmod(n, 2)
                    ins = mm(gd[:], w2_s[:, e, k, m * P:m * P + P], hc[:, e, k, :], start=False, stop=(n == 15))
                    if n == 15:
                        ins.then_inc(sem["gd_full"], 1)

                def experts_up(c):
                    for e in range(4 * (c - 2), 4 * (c - 2) + 4):
                        for m in range(2):
                            to_act(c, ("h", e, m), [(w1_s[:, e, k, m * P:m * P + P], tn[:, k, :]) for k in range(KT)])
                        to_dve(c, ("bc", e), [(sele_s[:, e, :], combT[:])])

                for c in range(CH):
                    par, late = (c + 1) % 2, on(LATE[c], i)
                    for u in range(UNITS):
                        if on(0, i):
                            if u == 0:
                                bcast(c, 0)
                            if u + 1 < UNITS:
                                bcast(c, u + 1)
                        if c == 0 and on(2, i) and u in DOWN_SLOTS:
                            down(0, DOWN_SLOTS.index(u) - 1)
                        if on(prep(c), i):
                            if u == 6:
                                pe.wait_ge(*after("xc", i, c))
                                to_act(c, "DT", [(wdt_s[:], xcs[:, par, :])])
                            if u == 7:
                                to_act(c, "B", [(wb_s[:], xcs[:, par, :])])
                            if u == 8:
                                to_act(c, "C", [(wc_s[:], xcs[:, par, :])])
                        if late and c in (0, 2):
                            if u == 9:
                                pe.wait_ge(*after("yg", i, 3 if c == 0 else 1, back=1 if c == 0 else 0))
                                pe.wait_ge(*ga_free(i, (c, "outp")))
                                for k in range(2):
                                    ins = mm(ga2[ga_bank((c, "outp"))][k * DM:(k + 1) * DM, :], wo_s[:], yg[:, k, :], start=True, stop=True)
                                ins.then_inc(sem["ga_full"], 1)
                            if u == 11:
                                pe.wait_ge(*after("ga_evac", i, (c, "outp")))
                                to_act(c, "var", [(mean64_s[:], sq2[:, 0, :])])
                        if late and c in (1, 3) and u == 0:
                            pe.wait_ge(*after("ga_evac", i, (c - 1, ("F", 1, 1))))
                            pe.wait_ge(*gd_free(i, (c, "fc2")))
                            for k in range(2):
                                for hh in range(2):
                                    ins = mm(gd[hh * DM:(hh + 1) * DM, :], wf2_s[:, k, :], gl[:, hh, k, :], start=(k == 0), stop=(k == 1))
                            ins.then_inc(sem["gd_full"], 1)
                        if c == 1 and on(1, i):
                            if u in (2, 4):
                                m = (u - 2) // 2
                                if m == 0:
                                    pe.wait_ge(*after("gd_evac", i, (1, "fc2")))
                                to_act(c, f"wout{m}", [(wout_s[:, k, m * P:m * P + P], skip[:, k, :]) for k in range(KT)])
                            if u == 12:
                                pe.wait_ge(*after("x1", i, 0))
                                to_dve(c, "mean", [(mean256_s[:], x1[:, k, :]) for k in range(KT)])
                            if u == 15:
                                pe.wait_ge(*after("tail_sq", i, 0))
                                to_act(c, "tvar", [(mean256_s[:], sq2[:, k, :]) for k in range(KT)])
                        if c == 2 and on(-1, i):
                            if u == 1:
                                pe.wait_ge(*after("xt", i, 0))
                                to_dve(c, "hmean", [(mean256_s[:], xn[:, k, :]) for k in range(KT)])
                            if u == 4:
                                pe.wait_ge(*after("head_sq", i, 0))
                                to_act(c, "hvar", [(mean256_s[:], sq2[:, k, :]) for k in range(KT)])
                        if on(0, i) and u in (6, 10, 14):
                            reduce(c, u // 4 - 1)
                    cx = (c + 2) % CH

                    def first_x():
                        if on(prep_in(c), i):
                            if c == 2:
                                pe.wait_ge(*after("xs", i, 0))
                            to_act(c, "X", [(wx_s[:, cx % 2, :], xs[:, cx // 2, :])])

                    def then_z():
                        if on(prep_in(c), i):
                            to_act(c, "Z", [(wz_s[:, cx % 2, :], xs[:, cx // 2, :])])

                    first_x()
                    if late and c in (0, 2):
                        pe.wait_ge(*after("yn_aff", i, c))
                        for hh in range(2):
                            for m in range(2):
                                to_act(c, ("F", hh, m), [(wf1_s[:, hh, m * P:m * P + P], yn[:])])
                    if on(0, i):
                        reduce(c, 3)
                    then_z()
                    if c == 0 and on(2, i):
                        for n in range(len(DOWN_SLOTS) - 1, 16):
                            down(0, n)
                    if c == 1 and on(2, i):
                        for n in range(-1, 8):
                            down(1, n)
                    if c == 1 and on(1, i):
                        pe.wait_ge(*after("tn", i, 0))
                        pe.wait_ge(*ga_free(i, (1, "router")))
                        for t in range(4):
                            for k in range(KT):
                                ins = mm(ga2[ga_bank((1, "router"))][:, t * NE:(t + 1) * NE], tn[:, k, t * P:(t + 1) * P],
                                         router_s[:, k, :], start=(k == 0), stop=(k == KT - 1))
                        ins.then_inc(sem["ga_full"], 1)
                    if c == 1 and on(2, i):
                        for n in range(8, 16):
                            down(1, n)
                    if c == 1 and on(1, i):
                        pe.wait_ge(*after("topk", i, TOPK_STEPS - 1))
                        pe.wait_ge(*ga_free(i, (1, "combT")))
                        for t in range(4):
                            ins = nc.tensor.transpose(transposed(ga2[ga_bank((1, "combT"))])[:, t * P:(t + 1) * P], c24[:, t, :], ident_s[:])
                        ins.then_inc(sem["ga_full"], 1)
                    if c >= 2 and on(1, i):
                        if c == 2:
                            pe.wait_ge(*after("ga_evac", i, (1, "combT")))
                        experts_up(c)

            rounds(pe, one)

        @block.scalar
        def _(act):
            f = nc.scalar.activation
            act.preload_act_table_set("natural_log_exp_and_others")
            act.wait_ge(ready, READY)
            f(col("A", 0, UNITS), col("A_log", 0, UNITS), ACT.Exp).then_inc(setup_act, 1)
            act.wait_ge(setup_mm, 1)
            f(wdt_s[:], gd[:, 0:P], ACT.Copy).then_inc(setup_act, 1)
            f(col("bn_s", 0, KT), col("bn_var", 0, KT), ACT.Ln, bias=col("eps")).then_inc(setup_act, 1)
            act.wait_ge(setup_act, 3)
            f(col("bn_s", 0, KT), col("bn_s", 0, KT), ACT.Exp, scale=-0.5).then_inc(setup_act, 1)
            act.wait_ge(derived, 1)

            def halo_at(slot, cn, ahead):
                start = (slot + ahead) * (CH * (KC - 1)) + cn * (KC - 1)
                return halo[:, start:start + KC - 1] if isinstance(slot, int) else halo[:, bass.ds(start, KC - 1)]

            def one(i):
                def full(c, name):
                    act.wait_ge(*after("ga_full", i, (c, name)))
                    return ga2[ga_bank((c, name))][:]

                def rstd(c, name, eps, done):
                    f(rs2[:], full(c, name), ACT.Ln, bias=col(eps)).then_inc(sem["ga_evac"], 1)
                    act.wait_ge(*after("ga_evac", i, (c, name)))
                    f(rs2[:], rs2[:], ACT.Exp, scale=-0.5).then_inc(sem[done], 1)

                def exp(c, u):
                    n = c * UNITS + u
                    act.wait_ge(*after("bcast_a", i, (c, u)))
                    f(pa[n % 2][:], pa[n % 2][:], ACT.Exp, scale=col("A", group(u)[2])).then_inc(sem["exp"], 1)

                for c in range(CH):
                    par, late = (c + 1) % 2, on(LATE[c], i)
                    for u in range(UNITS):
                        if on(0, i):
                            if u == 0:
                                exp(c, 0)
                            if u + 1 < UNITS:
                                exp(c, u + 1)
                        if on(prep(c), i):
                            if u == 1:
                                act.wait_ge(*after("conv", i, ((c - 1) % CH, KC - 2), back=1 if c == 0 else 0))
                                act.wait_ge(*after("ga_evac", i, ((c - 1) % CH, "Z"), back=1 if c == 0 else 0))
                                f(ge[:], za[:], ACT.Exp, scale=-1.0).then_inc(sem["neg_exp"], 1)
                            if u == 3:
                                act.wait_ge(*after("cap", i, c))
                                f(ge[:], ge[:], ACT.Ln, bias=col("one")).then_inc(sem["ln_g"], 1)
                            if u == 4:
                                act.wait_ge(*after("ln_g", i, c))
                                f(ge[:], ge[:], ACT.Exp, scale=-1.0).then_inc(sem["gate"], 1)
                            if u == 7:
                                act.wait_ge(*after("zs", i, c))
                                dt_raw = full(c, "DT")
                                f(v, dt_raw, ACT.Identity, bias=col("b_dt"))
                                f(ev, dt_raw, ACT.Abs, bias=col("b_dt")).then_inc(sem["ga_evac"], 1)
                            if u == 8:
                                f(bs[:, par, :], full(c, "B"), ACT.Copy).then_inc(sem["ga_evac"], 1)
                                act.wait_ge(*after("ga_evac", i, (c, "DT")))
                                f(ev, ev, ACT.Exp, scale=-1.0).then_inc(sem["sp_exp"], 1)
                            if u == 9:
                                f(cs[:, par, :], full(c, "C"), ACT.Copy).then_inc(sem["ga_evac"], 1)
                                act.wait_ge(*after("sp_exp", i, c))
                                f(lnu, ev, ACT.Ln, bias=col("one")).then_inc(sem["sp_ln"], 1)
                        if late and c in (0, 2):
                            if u == 10:
                                y = full(c, "outp")
                                f(yn[:], y, ACT.Copy)
                                f(sq2[:, 0, :], y, ACT.Square).then_inc(sem["ga_evac"], 1)
                            if u == 12:
                                rstd(c, "var", "eps", "rstd")
                            if u == 15:
                                act.wait_ge(*after("yn", i, c))
                                f(yn[:], yn[:], ACT.Identity, scale=col("g1"), bias=col("b1")).then_inc(sem["yn_aff"], 1)
                        if c == 1 and on(1, i):
                            if u in (3, 5):
                                m = (u - 3) // 2
                                y = full(c, f"wout{m}")
                                f(oc[:, m, :], y, ACT.Identity, scale=col("bn_s", m), bias=col("bn_t", m))
                                f(eo[:, m, :], y, ACT.Exp, scale=col("bn_ns", m), bias=col("bn_nt", m)).then_inc(sem["ga_evac"], 1)
                            if u == 7:
                                act.wait_ge(*after("cap_o", i, 0))
                                f(eo, eo, ACT.Ln, bias=col("one")).then_inc(sem["ln_o"], 1)
                            if u == 8:
                                act.wait_ge(*after("ln_o", i, 0))
                                f(eo, eo, ACT.Exp, scale=-1.0).then_inc(sem["gate_o"], 1)
                            if u == 14:
                                act.wait_ge(*after("gd_evac", i, (1, "mean")))
                                f(sq2[:], tn[:], ACT.Square).then_inc(sem["tail_sq"], 1)
                        if c == 2 and on(-1, i):
                            if u == 2:
                                act.wait_ge(*after("gd_evac", i, (2, "hmean")))
                                f(sq2[:], xn[:], ACT.Square).then_inc(sem["head_sq"], 1)
                            if u == 5:
                                rstd(c, "hvar", "head_add", "rstd_h")
                        if c == 2 and u == 3 and on(0, i):
                            act.wait_ge(*after("xs", i, 0, back=1))
                            for k in range(KT):
                                f(skip[:, k, :], xs[:, k, :], ACT.Identity, scale=col("skip"), bias=col("b_fc2")).then_inc(sem["skip_in"], 1)
                        if c == 2 and u == 8 and on(-1, i):
                            act.wait_ge(*after("xn", i, 0))
                            act.wait_ge(*after("skip_in", i, 1))
                            for k in range(KT):
                                ins = f(xs[:, k, :], xn[:, k, :], ACT.Identity, scale=col("g_head", k), bias=col("b", k))
                            ins.then_inc(sem["xs"], 1)
                    j, cx = i + (1 if c >= 2 else 0), (c + 2) % CH
                    if c == 1 and on(1, i):
                        rstd(c, "tvar", "eps", "rstd_t")
                    if on(prep_in(c), i):
                        x_in = full(c, "X")
                        act.wait_ge(*after("dt", i, c))
                        act.wait_ge(*after("halo", i, (c - 1) % CH, back=1 if c == 0 else 0))
                        f(xh[:, KC - 1:], x_in, ACT.Copy)
                        f(acc, x_in, ACT.Identity, scale=col("conv", KC - 1), bias=col("b_conv"))
                        f(halo_at(j % PER_IMAGE, cx, 1), ga2[ga_bank((c, "X"))][:, T - KC + 1:T], ACT.Copy).then_inc(sem["ga_evac"], 1)
                        f(xh[:, 0:KC - 1], halo_at(j % PER_IMAGE, cx, 0), ACT.Copy).then_inc(sem["halo"], 1)
                    if on(prep(c), i):
                        act.wait_ge(*after("dt", i, c))
                        act.wait_ge(*after("dtx", i, c))
                        f(part[0][:], v2[:], ACT.Copy).then_inc(sem["hi"], 1)
                    if late and c in (0, 2):
                        for hh in range(2):
                            for m in range(2):
                                f(gl[:, hh, m, :], full(c, ("F", hh, m)), ACT.Gelu, bias=col("b_fc1", m)).then_inc(sem["ga_evac"], 1)
                    if on(prep(c), i):
                        act.wait_ge(*after("rest", i, c))
                        f(part[1][:], v2[:], ACT.Copy).then_inc(sem["mid"], 1)
                    if on(prep_in(c), i):
                        act.wait_ge(*after("dt", i, c))
                        f(zc, full(c, "Z"), ACT.Copy).then_inc(sem["ga_evac"], 1)
                    if c == 1 and on(1, i):
                        y = ga2[ga_bank((1, "router"))][:, 0:4 * NE].rearrange("p (t e) -> p t e", e=NE)
                        full(c, "router")
                        f(lg[:], y, ACT.Copy).then_inc(sem["ga_evac"], 1)
                        act.wait_ge(*after("topk", i, 8))
                        f(pr[:, 1, :], pr[:, 0, :], ACT.Exp).then_inc(sem["topk_exp"], 1)
                        y = transposed(ga2[ga_bank((1, "combT"))])
                        full(c, "combT")
                        f(combT[:], y, ACT.Copy)
                        f(combTf[:], y, ACT.Copy).then_inc(sem["ga_evac"], 1)
                    if c >= 2 and on(1, i):
                        for e in range(4 * (c - 2), 4 * (c - 2) + 4):
                            for m in range(2):
                                f(hc[:, e, m, :], full(c, ("h", e, m)), ACT.Gelu, bias=col("moe_b1", 2 * e + m)).then_inc(sem["ga_evac"], 1)
                    if c != 1:
                        act.preload_act_table_set("natural_log_exp_and_others")

            rounds(act, one)

        @block.vector
        def _(dve):
            tt, ts, stt = nc.vector.tensor_tensor, nc.vector.tensor_scalar, nc.vector.scalar_tensor_tensor
            nc.vector.memset(state[:], 0.0)
            nc.vector.memset(halo[:], 0.0)
            nc.vector.memset(col("one"), 1.0)
            nc.vector.memset(col("eps"), LN_EPS)
            nc.vector.memset(col("head_add"), HEAD_ADD).then_inc(ready, 1)
            chain = [0]

            def link(ins):
                chain[0] += 1
                ins.then_inc(setup_dve, 1)
                dve.wait_ge(setup_dve, chain[0])

            dve.wait_ge(ready, READY)
            dve.wait_ge(setup_act, 4)
            link(ts(col("A", 0, UNITS), col("A", 0, UNITS), -1.0, None, ALU.mult))
            link(ts(col("g_head", 0, KT), col("g", 0, KT), HEAD_SCALE, None, ALU.mult))
            link(ts(col("bn_v", 0, KT), col("bn_var", 0, KT), LN_EPS, -0.5, ALU.add, ALU.mult))
            link(tt(col("bn_v", 0, KT), col("bn_v", 0, KT), col("bn_s", 0, KT), ALU.mult))
            link(tt(col("bn_v", 0, KT), col("bn_v", 0, KT), col("bn_s", 0, KT), ALU.mult))
            link(ts(col("bn_v", 0, KT), col("bn_v", 0, KT), 1.5, None, ALU.add))
            link(tt(col("bn_s", 0, KT), col("bn_s", 0, KT), col("bn_v", 0, KT), ALU.mult))
            link(tt(col("bn_s", 0, KT), col("bn_s", 0, KT), col("bn_g", 0, KT), ALU.mult))
            link(tt(col("bn_t", 0, KT), col("bn_s", 0, KT), col("bn_mean", 0, KT), ALU.mult))
            link(tt(col("bn_t", 0, KT), col("bn_b", 0, KT), col("bn_t", 0, KT), ALU.subtract))
            link(ts(col("bn_ns", 0, KT), col("bn_s", 0, KT), -1.0, None, ALU.mult))
            link(ts(col("bn_nt", 0, KT), col("bn_t", 0, KT), -1.0, None, ALU.mult))
            link(nc.vector.reduce_sum(wo_mean[:], wo_s[:], axis=AX_X))
            link(ts(wo_mean[:], wo_mean[:], 1.0 / DM, None, ALU.mult))
            link(ts(wo_s[:], wo_s[:], wo_mean[:, 0:1], None, ALU.subtract))
            dve.sem_inc(derived, 1)

            def state_at(slot, n):
                start = slot * (CH * UNITS) + n
                return state[:, start:start + 1] if isinstance(slot, int) else state[:, bass.ds(start, 1)]

            def one(i):
                def weight(c, u):
                    n = c * UNITS + u
                    dve.wait_ge(*after("bcast_b", i, (c, u)))
                    if u == 0:
                        was = (c - 1) % CH
                        dve.wait_ge(*after("ga_evac", i, (was, "B"), back=1 if c == 0 else 0))
                    tt(bx[:, n % 3, :], pb[n % 2][:], bs[:, c % 2, :], ALU.mult).then_inc(sem["bx"], 1)

                for c in range(CH):
                    par, late = (c + 1) % 2, on(LATE[c], i)
                    for u in range(UNITS):
                        n = c * UNITS + u
                        if on(0, i):
                            if u == 0:
                                weight(c, 0)
                            if u + 1 < UNITS:
                                weight(c, u + 1)
                            dve.wait_ge(*after("exp", i, (c, u)))
                            dve.wait_ge(*after("bx", i, (c, u)))
                            nc.vector.tensor_tensor_scan(h[:, n % RING, :], pa[n % 2][:], bx[:, n % 3, :], state_at(i % PER_IMAGE, n),
                                                         ALU.mult, ALU.add).then_inc(sem["scan"], 1)
                        if on(prep(c), i):
                            if u == 2:
                                dve.wait_ge(*after("neg_exp", i, c))
                                ts(ge[:], ge[:], EXP_CAP, None, ALU.min).then_inc(sem["cap"], 1)
                            if u == 5:
                                dve.wait_ge(*after("gate", i, c))
                                tt(xcs[:, par, :], acc, ge[:, 1, :], ALU.mult).then_inc(sem["xc"], 1)
                            if u == 8:
                                dve.wait_ge(*after("ga_evac", i, (c, "DT")))
                                ts(v, v, 0.0, None, ALU.max).then_inc(sem["sp_max"], 1)
                            if u == 9:
                                dve.wait_ge(*after("sp_exp", i, c))
                                ts(dr, ev, 1.0, 1.0, ALU.add, ALU.subtract).then_inc(sem["sp_round"], 1)
                        if c in (1, 3) and u == 1 and late:
                            pair = 1 if c == 1 else 0
                            dve.wait_ge(*after("gd_full", i, (c, "fc2")))
                            dve.wait_ge(*after("skip_in", i, 1, back=1 if c == 1 else 0))
                            tt(skip[:, pair, :], skip[:, pair, :], gd[:], ALU.add).then_inc(sem["gd_evac"], 1)
                        if c == 1 and on(1, i):
                            if u == 6:
                                dve.wait_ge(*after("ga_evac", i, (1, "wout1")))
                                ts(eo, eo, EXP_CAP, None, ALU.min).then_inc(sem["cap_o"], 1)
                            if u == 9:
                                dve.wait_ge(*after("gate_o", i, 0))
                                tt(oc, oc, eo, ALU.mult).then_inc(sem["o"], 1)
                            if u == 13:
                                dve.wait_ge(*after("gd_full", i, (1, "mean")))
                                dve.wait_ge(*after("fin", i, 0, back=1))
                                for m in range(KT):
                                    ins = tt(tn[:, m, :], x1[:, m, :], gd[:], ALU.subtract)
                                ins.then_inc(sem["gd_evac"], 1)
                        if c == 2 and on(-1, i):
                            if u == 1:
                                dve.wait_ge(*after("gd_full", i, (2, "hmean")))
                                for m in range(KT):
                                    ins = tt(xn[:, m, :], xn[:, m, :], gd[:], ALU.subtract)
                                ins.then_inc(sem["gd_evac"], 1)
                            if u == 6:
                                dve.wait_ge(*after("rstd_h", i, 0))
                                for m in range(KT):
                                    ins = tt(xn[:, m, :], xn[:, m, :], rs2[:], ALU.mult)
                                ins.then_inc(sem["xn"], 1)
                    if on(prep(c), i):
                        dve.wait_ge(*after("sp_ln", i, c))
                        dve.wait_ge(*after("sp_err", i, c))
                        tt(lnu, lnu, dr, ALU.add).then_inc(sem["sp_sum"], 1)
                        dve.wait_ge(*after("sp_sum", i, c))
                        dve.wait_ge(*after("sp_max", i, c))
                        tt(v2[:, 0, :], lnu, v, ALU.add).then_inc(sem["dt"], 1)
                    if c == 1 and on(1, i):
                        dve.wait_ge(*after("rstd_t", i, 0))
                        for m in range(KT):
                            ins = tt(tn[:, m, :], tn[:, m, :], rs2[:], ALU.mult)
                        ins.then_inc(sem["tn"], 1)
                    if on(prep(c), i):
                        dve.wait_ge(*after("hi", i, c))
                        tt(v2[:], v2[:], part[0][:], ALU.subtract).then_inc(sem["rest"], 1)
                    for k in range(KC - 1):
                        if on(prep_in(c), i):
                            if k == 0:
                                dve.wait_ge(*after("halo", i, c))
                            else:
                                dve.wait_ge(*after("conv", i, (c, k - 1)))
                            stt(acc, xh[:, k:k + T], col("conv", k), acc, ALU.mult, ALU.add).then_inc(sem["conv"], 1)
                        if k == 1 and on(prep(c), i):
                            dve.wait_ge(*after("mid", i, c))
                            tt(part[2][:], v2[:], part[1][:], ALU.subtract).then_inc(sem["lo"], 1)
                    if on(0, i):
                        dve.wait_ge(*after("yred", i, c))
                        stt(yg[:, c % 2, :], xcs[:, c % 2, :], col("D"), py[:], ALU.mult, ALU.add).then_inc(sem["yd"], 1)
                    if c == 1 and on(1, i):
                        topk(i)
                    if c < 2 and on(2, i):
                        dve.wait_ge(*after("gd_full", i, (c, "down")))
                        dve.wait_ge(*after("stored", i, c, back=1))
                        if c == 0:
                            dve.wait_ge(*after("fin", i, 0, back=1))
                        tt(fin[:, c, :], fin[:, c, :], gd[:], ALU.add).then_inc(sem["gd_evac"], 1)
                    if c >= 2 and on(1, i):
                        for e in range(4 * (c - 2), 4 * (c - 2) + 4):
                            dve.wait_ge(*after("gd_full", i, (c, ("bc", e))))
                            dve.wait_ge(*after("ga_evac", i, (c, ("h", e, 1))))
                            for m in range(2):
                                ins = tt(hc[:, e, m, :], hc[:, e, m, :], gd[:], ALU.mult)
                            ins.then_inc(sem["gd_evac"], 1)

            def topk(i):
                step = [0]

                def mark(ins):
                    ins.then_inc(sem["topk"], 1)
                    step[0] += 1

                def then(ins):
                    mark(ins)
                    dve.wait_ge(*after("topk", i, step[0] - 1))

                dve.wait_ge(*after("ga_evac", i, (1, "router")))
                dve.sem_inc(unheeded, 1)
                for t in range(4):
                    mark(nc.vector.max(mx[:, t, :], lg[:, t, :]))
                dve.wait_ge(*after("topk", i, 3))
                dve.sem_inc(unheeded, 1)
                for t in range(4):
                    mark(nc.vector.max_index(ix[:, t, :], mx[:, t, :], lg[:, t, :]))
                mark(tt(pr[:, 0, :], mx[:, :, 1], mx[:, :, 0], ALU.subtract))
                dve.wait_ge(*after("topk", i, 7))
                then(nc.vector.tensor_copy(ixf[:], ix[:, :, 0:2]))
                for k in range(2):
                    mark(tt(cmp[:, k, :, :], iota_s[:], ixf[:, :, k:k + 1].to_broadcast([P, 4, NE]), ALU.is_equal))
                dve.wait_ge(*after("topk_exp", i, 0))
                then(ts(pr[:, 2, :], pr[:, 1, :], 1.0, None, ALU.add))
                then(nc.vector.reciprocal(pr[:, 2, :], pr[:, 2, :]))
                then(tt(pr[:, 3, :], pr[:, 2, :], pr[:, 1, :], ALU.mult))
                mark(tt(cmp[:, 0, :, :], cmp[:, 0, :, :], pr[:, 2, :].unsqueeze(2).to_broadcast([P, 4, NE]), ALU.mult))
                then(tt(cmp[:, 1, :, :], cmp[:, 1, :, :], pr[:, 3, :].unsqueeze(2).to_broadcast([P, 4, NE]), ALU.mult))
                then(tt(comb[:], cmp[:, 0, :, :], cmp[:, 1, :, :], ALU.add))
                then(nc.vector.tensor_copy(c24[:, :, 0:NE], comb[:]))
                then(tt(comb[:], comb[:], c24[:, :, 0:NE], ALU.subtract))
                then(nc.vector.tensor_copy(c24[:, :, NE:2 * NE], comb[:]))
                mark(tt(c24[:, :, 2 * NE:3 * NE], comb[:], c24[:, :, NE:2 * NE], ALU.subtract))
                assert step[0] == TOPK_STEPS

            rounds(dve, one)

        @block.gpsimd
        def _(pool):
            tt = nc.gpsimd.tensor_tensor
            pool.wait_ge(derived, 1)

            def state_at(slot, n):
                start = (slot + 1) * (CH * UNITS) + n
                return state[:, start:start + 1] if isinstance(slot, int) else state[:, bass.ds(start, 1)]

            def one(i):
                for c in range(CH):
                    par, late = (c + 1) % 2, on(LATE[c], i)
                    for u in range(UNITS):
                        n = c * UNITS + u
                        if on(0, i):
                            pool.wait_ge(*after("scan", i, (c, u)))
                            nc.gpsimd.tensor_copy(state_at(i % PER_IMAGE, n), h[:, n % RING, T - 1:T]).then_inc(sem["saved"], 1)
                            pool.wait_ge(*after("saved", i, (c, u)))
                            tt(h[:, n % RING, :], h[:, n % RING, :], cs[:, c % 2, :], ALU.mult).then_inc(sem["prod"], 1)
                        if on(prep(c), i):
                            if u == 5:
                                pool.wait_ge(*after("gate", i, c))
                                tt(zs[:, par, :], zc, ge[:, 0, :], ALU.mult).then_inc(sem["zs"], 1)
                            if u == 10:
                                pool.wait_ge(*after("sp_round", i, c))
                                tt(dr, ev, dr, ALU.subtract).then_inc(sem["sp_err"], 1)
                        if late and c in (0, 2) and u == 13:
                            pool.wait_ge(*after("rstd", i, c))
                            tt(yn[:], yn[:], rs2[:], ALU.mult).then_inc(sem["yn"], 1)
                        if c == 1 and on(1, i) and u == 9:
                            pool.wait_ge(*after("o", i, 0))
                            pool.wait_ge(*after("xr", i, 0))
                            tt(x1[:], x1[:], oc, ALU.add).then_inc(sem["x1"], 1)
                    if on(prep(c), i):
                        pool.wait_ge(*after("dt", i, c))
                        tt(v2[:, 1, :], v2[:, 0, :], xcs[:, par, :], ALU.mult).then_inc(sem["dtx"], 1)
                    if on(0, i):
                        pool.wait_ge(*after("yd", i, c))
                        tt(yg[:, c % 2, :], yg[:, c % 2, :], zs[:, c % 2, :], ALU.mult).then_inc(sem["yg"], 1)
                    if c == 1 and on(1, i):
                        pool.wait_ge(*after("tn", i, 0))
                        pool.wait_ge(*after("stored", i, 1))
                        tt(fin[:], x1[:], tn[:], ALU.add).then_inc(sem["fin"], 1)

            rounds(pool, one)


def kernel(**inputs):
    import ml_dtypes
    import numpy as np
    import concourse.bacc as bacc
    from concourse.bass_utils import run_bass_kernel_spmd

    g = {k: np.asarray(v) for k, v in inputs.items()}
    L0 = {k[len("L0_conv_"):]: v for k, v in g.items() if k.startswith("L0_conv_")}
    FF = {k[len("L0_ffn_"):]: v for k, v in g.items() if k.startswith("L0_ffn_")}
    f32, bf = np.float32, ml_dtypes.bfloat16

    def halves(v):
        return v.reshape(KT, P).T

    def twice(v):
        return np.concatenate([v, v])[:, None]

    small = np.concatenate([
        L0["W_conv"].reshape(DI, KC), L0["b_conv"][:, None], L0["b_dt"][:, None], L0["D_par"][:, None],
        halves(L0["g_norm"]), halves(L0["b_norm"]), twice(L0["g_norm1"]), twice(L0["b_norm1"]),
        L0["b_fc1"].reshape(2, P).T, twice(L0["b_fc2"]), np.broadcast_to(L0["skip_scale"], (P, 1)),
        halves(L0["bn_g"]), halves(L0["bn_b"]), halves(L0["bn_mean"]), halves(L0["bn_var"]),
        FF["b1"].reshape(NE, 2, P).transpose(2, 0, 1).reshape(P, 2 * NE),
        L0["A_log"].reshape(UNITS, P).T], 1)

    def at_half(w):
        o = np.zeros((P, 2, w.shape[1]), w.dtype)
        for k in range(2):
            o[k * DM:(k + 1) * DM, k] = w
        return o

    W_in, Wx = L0["W_in"], L0["W_xproj"]
    wout = L0["W_out"].T.reshape(DM, CH, C).transpose(1, 0, 2).reshape(KT, P, C).transpose(1, 0, 2)
    experts = lambda w: w.reshape(NE, KT, P, C).transpose(2, 0, 1, 3)
    p = np.arange(P)
    red = np.zeros((P, 4, 32), f32)
    sel = np.zeros((PARTS, 32, 4, P), f32)
    for r in range(4):
        red[p, r, 8 * r + p // NS] = 1
        sel[:, 8 * r + p // NS, r, p] = 1
    sele = np.zeros((PARTS, NE, NE, P), f32)
    for e in range(NE):
        sele[:, e, e, :] = 1
    arrays = dict(
        x=g["x"].reshape(B, KT, P, PER_IMAGE, T).transpose(0, 3, 2, 1, 4).reshape(TILES, P, KT, T),
        small=small, wx=at_half(W_in[:DI].T), wz=at_half(W_in[DI:].T), wdtl=Wx[:RK], wdtr=L0["W_dt"].T,
        wb=Wx[RK:RK + NS].T[:, p % NS], wc=Wx[RK + NS:].T[:, p % NS], wo=L0["W_outp"].T,
        wf1=at_half(L0["W_fc1"].T), wf2=L0["W_fc2"].T.reshape(2, P, DM).transpose(1, 0, 2), wout=wout, w1=experts(FF["w1"]), w2=experts(FF["w2"]),
        b2=np.concatenate([FF["b2"]] * PARTS), router=FF["router_w"].T.reshape(KT, P, NE).transpose(1, 0, 2),
        mean256=np.full((P, P), 1 / C, f32), mean64=np.kron(np.eye(2), np.full((DM, DM), 1 / DM)).astype(f32),
        red=red, iota=np.broadcast_to(np.arange(NE, dtype=f32), (P, 4, NE)),
        sel=sel.reshape(PARTS * 32, 4, P).astype(bf), sele=sele.reshape(PARTS * NE, NE, P).astype(bf),
        ident=np.eye(P, dtype=f32).astype(bf))
    arrays = {k: np.ascontiguousarray(v) for k, v in arrays.items()}

    nc = bacc.Bacc("TRN2", target_bir_lowering=False, num_devices=1)
    args = {k: nc.dram_tensor(f"in_{k}", v.shape, mybir.dt.from_np(v.dtype), kind="ExternalInput").ap() for k, v in arrays.items()}
    out = nc.dram_tensor("out_y", (TILES, P, KT, T), F32, kind="ExternalOutput").ap()
    build(nc, **args, out=out)
    r = run_bass_kernel_spmd(nc, [{f"in_{k}": v for k, v in arrays.items()}], core_ids=[0])
    y = np.asarray(r.results[0]["out_y"])
    return y.reshape(B, PER_IMAGE, P, KT, T).transpose(0, 3, 2, 1, 4).reshape(B, C, H, W)
```

```python
from contextlib import ExitStack

import concourse.bass as bass
from concourse import mybir

F32 = mybir.dt.float32
BF16 = mybir.dt.bfloat16
U32 = mybir.dt.uint32
ALU = mybir.AluOpType
ACT = mybir.ActivationFunctionType
AX_X = mybir.AxisListType.X

P = 128
B, C, H, W = 4, 256, 64, 64
L = H * W
T = 512
KT = C // P
TILES = B * L // T
PER_IMAGE = L // T
CH = 4
DM = C // CH
DI = 2 * DM
NS = 16
KC = 4
RK = 4
UNITS = DI * NS // P
JU = P // NS
NE = 8
PARTS = 3
RING = 8
LATE_SLOTS = [1, 2, 3, 4, 8, 9, 10, 11, 12, 13]
WEIGHT_SLOTS = [0, 2, 3, 5]
DOWN_SLOTS = [1, 2, 3, 4, 8, 9, 10, 11]
DOWN_3 = [9, 12, 12]
DOWN_1 = [8, 9, 10, 11, 12]
DOWN_2 = [0, 1, 1, 2, 4]
TOPK_STEPS = 22
LN_EPS = 1e-5
LNC_EPS = 1e-6
HEAD_ADD = LNC_EPS * LN_EPS / (1.0 + LN_EPS)
HEAD_SCALE = (1.0 + LN_EPS) ** -0.5
EXP_CAP = 2.0 ** 60

SMALL = dict(conv=KC, b_conv=1, b_dt=1, D=1, g=KT, b=KT, g1=1, b1=1, b_fc1=2, b_fc2=1, skip=1,
             bn_g=KT, bn_b=KT, bn_mean=KT, bn_var=KT, moe_b1=NE * 2, A_log=UNITS,
             A=UNITS, g_head=KT, bn_s=KT, bn_t=KT, bn_ns=KT, bn_nt=KT, bn_v=KT, one=1, eps=1, head_add=1)
LOADED = sum(list(SMALL.values())[:17])
COL, _at = {}, 0
for _name, _n in SMALL.items():
    COL[_name] = _at
    _at += _n
NSMALL = _at

def prep(c):
    return -1 if c == CH - 1 else 0


def prep_in(c):
    return -1 if c >= CH - 2 else 0


LATE = {0: 1, 1: 1, 2: 0, 3: 0}
_prep = [(c, prep(c)) for c in range(CH)]
_prep_in = [(c, prep_in(c)) for c in range(CH)]
_chunk = [(c, 0) for c in range(CH)]
_unit = [((c, u), 0) for c in range(CH) for u in range(UNITS)]
_four = [((c, k), 0) for c in range(CH) for k in range(UNITS // 4)]
_pairs = [(0, 1), (2, 0)]
_fc1 = [("F", h, m) for h in range(2) for m in range(2)]
_up = {2: [("h", e, m) for e in range(4) for m in range(2)]}
_late = [(n, e, m) for e in range(4, 8) for n, m in (("h", 0), ("h", 1), ("bc", 0))]
GA_ORDER = {0: ["outp", "var", "DT", "B", "C", "X", "Z"] + _fc1,
            1: ["wout0", "wout1", "DT", "B", "C", "mean", "X", "Z", "tvar", "router"],
            2: ["hmean", "DT", "combT", "B", "C", "hvar", "outp", "var", "X", "Z"] + _up[2][:4] + _fc1 + _up[2][4:],
            3: _late[:4] + ["DT", "B", "C"] + _late[4:10] + ["X", "Z"] + _late[10:]}


def _ga_lag(c, n):
    if n in ("DT", "B", "C"):
        return prep(c)
    if n in ("X", "Z"):
        return prep_in(c)
    if n in ("hvar", "hmean"):
        return -1
    if n in ("wout0", "wout1", "mean", "tvar", "router", "combT") or n[0] in ("h", "bc"):
        return 1
    return LATE[c]


_ga = [((c, n), _ga_lag(c, n)) for c in range(CH) for n in GA_ORDER[c]]
_gd = [((0, "down"), 2), ((1, "fc2"), 1), ((1, "down"), 2)] \
    + [((2, ("bc", e)), 1) for e in range(4)] + [((3, "fc2"), 0)]
EVENTS = dict(
    bcast_a=_unit, bcast_b=_unit, reduced=_four, ga_full=_ga, gd_full=_gd,
    ga_evac=_ga, exp=_unit, halo=_prep_in, neg_exp=_prep, ln_g=_prep, gate=_prep,
    ln_o=[(0, 1)], gate_o=[(0, 1)], rstd=_pairs, rstd_h=[(0, -1)], rstd_t=[(0, 1)], sp_exp=_prep, sp_ln=_prep,
    hi=_prep, mid=_prep, yn_aff=_pairs, skip_in=[(0, 0), (1, 0)], tail_sq=[(0, 1)], head_sq=[(0, -1)],
    xs=[(0, -1)], topk_exp=[(0, 1)], late_gelu=[(e, 1) for e in range(4, 8)],
    gd_evac=_gd, weighted=[(e, 2) for e in range(4, 8)], bx=_unit, scan=_unit, conv=[((c, k), lag) for c, lag in _prep_in for k in range(KC - 1)],
    yd=_chunk, cap=_prep, cap_o=[(0, 1)], sp_max=_prep, sp_round=_prep, xc=_prep, sp_sum=_prep, dt=_prep,
    rest=_prep, lo=_prep, centred=[(0, 1)], centred_h=[(0, -1)], o=[(0, 1)], x1=[(0, 1)], tn=[(0, 1)], xn=[(0, -1)], topk=[(k, 1) for k in range(TOPK_STEPS)],
    saved=_four, prod=_four, yg=_chunk, zs=_prep, sp_err=_prep, dtx=_prep, yn=_pairs, fin=[(0, 1)],
    xt=[(0, -1)], xr=[(0, 1)], stored=[(0, 2), (1, 2)],
    **{f"shuffle{p}{q}": [((c, k), lag) for c, lag in _prep if (c + 1) % 2 == p for k in range(PARTS)] for p in range(2) for q in range(4)},
)
DMA_COUNTED = ("xt", "xr", "stored") + tuple(f"shuffle{p}{q}" for p in range(2) for q in range(4))
FIRST, LAST = -1, TILES + 1
LOOP = (3, TILES - 1)


def on(lag, i):
    return not isinstance(i, int) or 0 <= i - lag < TILES


def _in_round(name, i):
    return [k for k, lag in EVENTS[name] if on(lag, i)]


def _before(name, i):
    return sum(len(_in_round(name, j)) for j in range(FIRST, i))


def count(name, i, key=None, back=0):
    n = len(EVENTS[name])
    unit = 16 if name in DMA_COUNTED else 1
    if isinstance(i, int):
        keys = _in_round(name, i - back)
        if key is None:
            return _before(name, i) * unit
        return (_before(name, i - back) + keys.index(key) + 1) * unit if key in keys else 0
    lags = {lag for _, lag in EVENTS[name]}
    assert not back or 2 not in lags or lags == {2}
    index = 0 if key is None else [k for k, _ in EVENTS[name]].index(key) + 1
    constant = _before(name, LOOP[0]) + index - n * back - n * LOOP[0]
    assert n * LOOP[0] + constant > 0
    return i * (n * unit) + constant * unit


GA_KEYS = [k for k, _ in _ga]
assert len(GA_KEYS) % 2 == 0


def ga_bank(key):
    return GA_KEYS.index(key) % 2


def ga_before(i, key):
    at = GA_KEYS.index(key)
    if not isinstance(i, int):
        return count("ga_evac", i, GA_KEYS[at - 2]) if at >= 2 else count("ga_evac", i) - (1 - at)
    for j in range(i, FIRST - 1, -1):
        for k in range(at - 2 if j == i else len(GA_KEYS) - 2 + at % 2, -1, -2):
            if GA_KEYS[k] in _in_round("ga_evac", j):
                return _before("ga_evac", j) + _in_round("ga_evac", j).index(GA_KEYS[k]) + 1
    return 0


def build(nc, x, small, wx, wz, wdtl, wdtr, wb, wc, wo, wf1, wf2, wout, w1, w2, b2, router,
          mean256, mean64, red, iota, sel, sele, ident, out):
    with ExitStack() as ctx:
        def sb(name, shape, dt=F32):
            return ctx.enter_context(nc.sbuf_tensor(name, shape, dt))

        def bank(name):
            return ctx.enter_context(nc.psum_tensor(name, [P, T], F32))

        sem = {name: ctx.enter_context(nc.semaphore(name)) for name in EVENTS}
        ready = ctx.enter_context(nc.semaphore("ready"))
        derived = ctx.enter_context(nc.semaphore("derived"))
        unheeded = ctx.enter_context(nc.semaphore("unheeded"))
        setup_mm = ctx.enter_context(nc.semaphore("setup_mm"))
        setup_act = ctx.enter_context(nc.semaphore("setup_act"))
        setup_dve = ctx.enter_context(nc.semaphore("setup_dve"))

        small_s = sb("small_s", [P, NSMALL])
        wx_s, wz_s = sb("wx_s", [P, 2, P]), sb("wz_s", [P, 2, P])
        wdtl_s, wdtr_s, wdt_s = sb("wdtl_s", [RK, P]), sb("wdtr_s", [RK, P]), sb("wdt_s", [P, P])
        wb_s, wc_s = sb("wb_s", [P, P]), sb("wc_s", [P, P])
        wo_s = sb("wo_s", [P, DM])
        wf1_s, wf2_s = sb("wf1_s", [P, 2, C]), sb("wf2_s", [P, 2, DM])
        wout_s = sb("wout_s", [P, KT, C])
        w1_s, w2_s = sb("w1_s", [P, NE, KT, C]), sb("w2_s", [P, NE, KT, C])
        b2_s, router_s = sb("b2_s", [PARTS * NE, C]), sb("router_s", [P, KT, NE])
        mean256_s, mean64_s = sb("mean256_s", [P, P]), sb("mean64_s", [P, P])
        red_s, iota_s = sb("red_s", [P, 4, 32]), sb("iota_s", [P, 4, NE])
        sel_s = sb("sel_s", [PARTS * 32, 4, P], BF16)
        sele_s, ident_s = sb("sele_s", [PARTS * NE, NE, P], BF16), sb("ident_s", [P, P], BF16)
        wo_mean = sb("wo_mean", [P, 1])

        def col(name, k=0, n=1):
            return small_s[:, COL[name] + k:COL[name] + k + n]

        state = sb("state", [P, (PER_IMAGE + 1) * CH * UNITS])
        halo = sb("halo", [P, (PER_IMAGE + 1) * CH * (KC - 1)])

        xn, xs = sb("xn_s", [P, KT, T]), sb("xs_s", [P, KT, T])
        sq2, rs2 = sb("sq2", [P, KT, T]), sb("rs2", [P, T])
        xh = sb("xh", [P, T + KC - 1])
        za, ge = sb("za", [P, 2, T]), sb("ge", [P, 2, T])
        zc, acc = za[:, 0, :], za[:, 1, :]
        v, dr, ev, lnu = za[:, 0, :], za[:, 1, :], ge[:, 0, :], ge[:, 1, :]
        xcs, zs = sb("xcs", [P, 2, T]), sb("zs_s", [P, 2, T])
        bs, cs = sb("bs", [P, 2, T]), sb("cs", [P, 2, T])
        v2 = sb("v2", [P, 2, T])
        part = [sb(n, [P, 2, T], BF16) for n in ("hi_s", "mid_s", "lo_s")]
        pd = [sb(f"pd{k}", [PARTS * 32, 2, 4, T], BF16) for k in range(2)]
        bx = sb("bx_s", [P, 3, T])
        h = sb("h", [P, RING, T])
        yg = sb("yg_s", [P, 2, T])
        yn, gl = sb("yn_s", [P, T]), sb("gl", [P, 2, 2, T])
        skip = sb("skip_s", [P, KT, T])
        oc, eo = gl[:, 0, :, :], gl[:, 1, :, :]
        late_w = [gl[:, e // 2, e % 2, :] for e in range(4)]
        x1, tn, fin = (sb(n, [P, KT, T]) for n in ("x1_s", "tn_s", "fin_s"))
        hc = sb("hc", [P, NE, 2, T])
        lg, mx, comb, cmp = sb("lg", [P, 4, NE]), sb("mx", [P, 4, 8]), sb("comb", [P, 4, NE]), sb("cmp", [P, 2, 4, NE])
        ix, ixf, pr = sb("ix", [P, 4, 8], U32), sb("ixf", [P, 4, 2]), sb("pr", [P, 4, 4])
        c24 = sb("c24", [P, 4, PARTS * NE], BF16)
        combT, combTf = sb("combT", [PARTS * NE, T], BF16), sb("combTf", [PARTS * NE, T])

        pa, pb = [bank(f"pa{k}") for k in range(2)], [bank(f"pb{k}") for k in range(2)]
        py, ga2, gd = bank("py"), [bank(f"ga{k}") for k in range(2)], bank("gd")

        loads = [(small_s[:, 0:LOADED], small), (wx_s, wx), (wz_s, wz), (wdtl_s, wdtl), (wdtr_s, wdtr),
                 (wb_s, wb), (wc_s, wc), (wo_s, wo), (wf1_s, wf1), (wf2_s, wf2), (wout_s, wout), (w1_s, w1),
                 (w2_s, w2), (b2_s, b2), (router_s, router), (mean256_s, mean256), (mean64_s, mean64),
                 (red_s, red), (iota_s, iota), (sel_s, sel), (sele_s, sele), (ident_s, ident)]
        READY = 16 * len(loads) + 1

        def met(name, n):
            return (sem[name], n) if not isinstance(n, int) or n > 0 else (derived, 1)

        def after(name, i, key, back=0):
            return met(name, count(name, i, key, back))

        def gd_free(i, key):
            return met("gd_evac", count("gd_evac", i, key) - 1)

        def ga_free(i, key):
            return met("ga_evac", ga_before(i, key))

        def rounds(eng, one):
            for i in range(FIRST, LOOP[0]):
                one(i)
            with eng.Fori(*LOOP) as i:
                one(i)
            for i in range(LOOP[1], LAST + 1):
                one(i)

        def group(u):
            q, r = u % 4, u // 4
            return q, r, 4 * q + r

        def transposed(bank_):
            return bank_[0:PARTS * NE, 0:T // 2].bitcast(BF16)

        block = ctx.enter_context(nc.Block())

        @block.sync
        def _(sp):
            for dst, src in loads:
                sp.dma_start(dst if isinstance(dst, bass.AP) else dst[:], src).then_inc(ready, 16)

            def one(i):
                if on(1, i):
                    sp.wait_ge(*after("fin", i, 0, back=1))
                    sp.dma_start(x1[:], tile(x, i - 1)).then_inc(sem["xr"], 16)
                if on(-1, i):
                    sp.wait_ge(*after("xs", i, 0, back=1))
                    sp.dma_start(xn[:], tile(x, i + 1)).then_inc(sem["xt"], 16)
                def store(m):
                    if on(2, i):
                        sp.wait_ge(*after("gd_evac", i, (m, "down")))
                        sp.dma_start(tile(out, i - 2)[:, m, :], fin[:, m, :]).then_inc(sem["stored"], 16)

                for c in range(CH):
                    if c == 2:
                        store(1)
                    if on(prep(c), i):
                        cn = (c + 1) % CH
                        for k, what in enumerate(("hi", "mid", "lo")):
                            sp.wait_ge(*after(what, i, c))
                            for q in range(4):
                                sp.dma_start(pd[cn % 2][32 * k:32 * k + 32, :, q, :],
                                             part[k][32 * q:32 * q + 32, :, :]).then_inc(sem[f"shuffle{cn % 2}{q}"], 16)
                    if c == 0:
                        store(0)

            def tile(dram, j):
                return dram[j] if isinstance(j, int) else dram[bass.ds(j, 1)].rearrange("a p k t -> (a p) k t")

            rounds(sp, one)
            sp.wait_ge(sem["stored"], 16 * KT * TILES)

        @block.tensor
        def _(pe):
            mm = nc.tensor.matmul
            pe.wait_ge(ready, READY)
            mm(gd[:, 0:P], wdtl_s[:], wdtr_s[:], start=True, stop=True).then_inc(setup_mm, 1)
            pe.wait_ge(derived, 1)

            def one(i):
                def bcast(c, u):
                    q, r, _ = group(u)
                    n = c * UNITS + u
                    if u < 4:
                        pe.wait_ge(*after(f"shuffle{c % 2}{q}", i, ((c - 1) % CH, PARTS - 1), back=1 if c == 0 else 0))
                    was, back = ((n - 2) // UNITS, 0) if n >= 2 else (CH - 1, 1)
                    pe.wait_ge(*after("bx", i, (was, (n - 2) % UNITS), back=back))
                    mm(pb[n % 2][:], sel_s[:, r, :], pd[c % 2][:, 1, q, :], start=True, stop=True).then_inc(sem["bcast_b"], 1)
                    pe.wait_ge(*after("exp", i, (was, (n - 2) % UNITS), back=back))
                    mm(pa[n % 2][:], sel_s[:, r, :], pd[c % 2][:, 0, q, :], start=True, stop=True).then_inc(sem["bcast_a"], 1)

                def reduce(c, k):
                    pe.wait_ge(*after("prod", i, (c, k)))
                    if k == 0:
                        pe.wait_ge(*after("yd", i, (c - 1) % CH, back=1 if c == 0 else 0))
                    for q in range(4):
                        n = c * UNITS + 4 * k + q
                        ins = mm(py[32 * q:32 * q + 32, :], red_s[:, k, :], h[:, n % RING, :], start=(k == 0), stop=(k == 3))
                    ins.then_inc(sem["reduced"], 1)

                def to_act(c, name, pieces):
                    bank_ = ga2[ga_bank((c, name))]
                    pe.wait_ge(*ga_free(i, (c, name)))
                    for k, (w, r) in enumerate(pieces):
                        ins = mm(bank_[:], w, r, start=(k == 0), stop=(k == len(pieces) - 1))
                    ins.then_inc(sem["ga_full"], 1)

                def to_dve(c, name, pieces):
                    pe.wait_ge(*gd_free(i, (c, name)))
                    for k, (w, r) in enumerate(pieces):
                        ins = mm(gd[:], w, r, start=(k == 0), stop=(k == len(pieces) - 1))
                    ins.then_inc(sem["gd_full"], 1)

                def down(m, n):
                    if n < 0:
                        pe.wait_ge(*(gd_free(i, (1, "down")) if m == 1 else after("gd_evac", i, (3, "fc2") if on(0, i) else (2, ("bc", 3)))))
                        mm(gd[:], b2_s[:, m * P:m * P + P], combTf[:], start=True, stop=False)
                        return
                    e, k = divmod(n, 2)
                    if m == 0 and e >= 4 and k == 0:
                        pe.wait_ge(*after("weighted", i, e))
                    ins = mm(gd[:], w2_s[:, e, k, m * P:m * P + P], hc[:, e, k, :], start=False, stop=(n == 15))
                    if n == 15:
                        ins.then_inc(sem["gd_full"], 1)

                def late_piece(n):
                    kind, e, m = _late[n]
                    if kind == "h":
                        up(3, e, m)
                    else:
                        to_act(3, _late[n], [(sele_s[:, e, :], combT[:])])

                def up(c, e, m):
                    to_act(c, ("h", e, m), [(w1_s[:, e, k, m * P:m * P + P], tn[:, k, :]) for k in range(KT)])

                for c in range(CH):
                    par, late, cx = (c + 1) % 2, on(LATE[c], i), (c + 2) % CH
                    for u in range(UNITS):
                        if on(0, i):
                            if u == 0:
                                bcast(c, 0)
                                bcast(c, 1)
                            if u + 2 < UNITS:
                                bcast(c, u + 2)
                            if u in (6, 10, 14):
                                reduce(c, u // 4 - 1)
                        if c == 0 and on(2, i) and u in DOWN_SLOTS:
                            down(0, DOWN_SLOTS.index(u) + 8)
                        if c == 3 and on(1, i) and u in DOWN_3:
                            for k in range(DOWN_3.count(u)):
                                down(0, DOWN_3.index(u) - 1 + k)
                        if c == 1 and on(2, i) and u in DOWN_1:
                            down(1, DOWN_1.index(u) - 1)
                        if c == 2 and on(2, i) and u in DOWN_2:
                            for k in range(DOWN_2.count(u)):
                                down(1, 16 - len(DOWN_2) + DOWN_2.index(u) + k)
                        if c == 3 and on(1, i) and u == 0:
                            to_dve(2, ("bc", 3), [(sele_s[:, 3, :], combT[:])])
                        if late and u == {1: 0, 3: 1}.get(c):
                            pe.wait_ge(*after("ga_evac", i, (c - 1, ("F", 1, 1))))
                            pe.wait_ge(*gd_free(i, (c, "fc2")))
                            for k in range(2):
                                for hh in range(2):
                                    ins = mm(gd[hh * DM:(hh + 1) * DM, :], wf2_s[:, k, :], gl[:, hh, k, :], start=(k == 0), stop=(k == 1))
                            ins.then_inc(sem["gd_full"], 1)
                        if late and u == {0: 0, 2: 11}.get(c):
                            pe.wait_ge(*after("yg", i, 3 if c == 0 else 1, back=1 if c == 0 else 0))
                            pe.wait_ge(*ga_free(i, (c, "outp")))
                            for k in range(2):
                                ins = mm(ga2[ga_bank((c, "outp"))][k * DM:(k + 1) * DM, :], wo_s[:], yg[:, k, :], start=True, stop=True)
                            ins.then_inc(sem["ga_full"], 1)
                        if late and u == {0: 3, 2: 13}.get(c):
                            pe.wait_ge(*after("ga_evac", i, (c, "outp")))
                            to_act(c, "var", [(mean64_s[:], sq2[:, 0, :])])
                        if c == 1 and on(1, i) and u in (3, 4):
                            m = u - 3
                            if m == 0:
                                pe.wait_ge(*after("gd_evac", i, (1, "fc2")))
                            to_act(c, f"wout{m}", [(wout_s[:, k, m * P:m * P + P], skip[:, k, :]) for k in range(KT)])
                        if c == 3 and on(1, i) and u in LATE_SLOTS:
                            late_piece(LATE_SLOTS.index(u))
                        if on(prep(c), i) and u == 5:
                            pe.wait_ge(*after("xc", i, c))
                            to_act(c, "DT", [(wdt_s[:], xcs[:, par, :])])
                        if c == 2 and on(1, i) and u == 5:
                            pe.wait_ge(*after("topk", i, TOPK_STEPS - 1))
                            pe.wait_ge(*ga_free(i, (2, "combT")))
                            for t in range(4):
                                ins = nc.tensor.transpose(transposed(ga2[ga_bank((2, "combT"))])[:, t * P:(t + 1) * P], c24[:, t, :], ident_s[:])
                            ins.then_inc(sem["ga_full"], 1)
                        if on(prep(c), i) and u == 6:
                            to_act(c, "B", [(wb_s[:], xcs[:, par, :])])
                        if c == 2 and on(-1, i) and u == 3:
                            pe.wait_ge(*after("xt", i, 0))
                            to_act(c, "hmean", [(mean256_s[:], xn[:, k, :]) for k in range(KT)])
                        if on(prep(c), i) and u == 7:
                            to_act(c, "C", [(wc_s[:], xcs[:, par, :])])
                        if c == 2 and on(-1, i) and u == 10:
                            pe.wait_ge(*after("head_sq", i, 0))
                            to_act(2, "hvar", [(mean256_s[:], sq2[:, k, :]) for k in range(KT)])
                        if c == 1 and on(1, i) and u == 13:
                            pe.wait_ge(*after("x1", i, 0))
                            to_act(c, "mean", [(mean256_s[:], x1[:, k, :]) for k in range(KT)])
                        if on(prep_in(c), i) and u == 14:
                            if c == 2:
                                pe.wait_ge(*after("xs", i, 0))
                            to_act(c, "X", [(wx_s[:, cx % 2, :], xs[:, cx // 2, :])])
                        if on(prep_in(c), i) and u == 14:
                            to_act(c, "Z", [(wz_s[:, cx % 2, :], xs[:, cx // 2, :])])
                    if c == 1 and on(2, i):
                        for n in range(len(DOWN_1) - 1, 6):
                            down(1, n)
                    if c == 1 and on(1, i):
                        pe.wait_ge(*after("tail_sq", i, 0))
                        to_act(c, "tvar", [(mean256_s[:], sq2[:, k, :]) for k in range(KT)])
                    if c == 1 and on(2, i):
                        for n in range(6, 8):
                            down(1, n)
                    if c == 2 and on(1, i):
                        for e in range(2):
                            up(c, e, 0)
                            up(c, e, 1)
                            to_dve(c, ("bc", e), [(sele_s[:, e, :], combT[:])])
                            if e == 0 and on(0, i):
                                reduce(c, 3)
                    if late and c in (0, 2):
                        pe.wait_ge(*after("yn_aff", i, c))
                        for hh in range(2):
                            for m in range(2):
                                to_act(c, ("F", hh, m), [(wf1_s[:, hh, m * P:m * P + P], yn[:])])
                    if c == 3 and on(1, i):
                        late_piece(10)
                        late_piece(11)
                        for n in range(len(DOWN_3) - 1, 6):
                            down(0, n)
                    if on(0, i) and not (c == 2 and on(1, i)):
                        reduce(c, 3)
                    if c == 3 and on(1, i):
                        for n in range(6, 8):
                            down(0, n)
                    if c == 1 and on(1, i):
                        pe.wait_ge(*after("tn", i, 0))
                        pe.wait_ge(*ga_free(i, (1, "router")))
                        for t in range(4):
                            for k in range(KT):
                                ins = mm(ga2[ga_bank((1, "router"))][:, t * NE:(t + 1) * NE], tn[:, k, t * P:(t + 1) * P],
                                         router_s[:, k, :], start=(k == 0), stop=(k == KT - 1))
                        ins.then_inc(sem["ga_full"], 1)
                    if c == 1 and on(2, i):
                        for n in range(8, 16 - len(DOWN_2)):
                            down(1, n)
                    if c == 2 and on(1, i):
                        for e in range(2, 4):
                            up(c, e, 0)
                            up(c, e, 1)
                            if e < 3:
                                to_dve(c, ("bc", e), [(sele_s[:, e, :], combT[:])])

            rounds(pe, one)

        @block.scalar
        def _(act):
            f = nc.scalar.activation
            act.preload_act_table_set("natural_log_exp_and_others")
            act.wait_ge(ready, READY)
            f(col("A", 0, UNITS), col("A_log", 0, UNITS), ACT.Exp).then_inc(setup_act, 1)
            act.wait_ge(setup_mm, 1)
            f(wdt_s[:], gd[:, 0:P], ACT.Copy).then_inc(setup_act, 1)
            f(col("bn_s", 0, KT), col("bn_var", 0, KT), ACT.Ln, bias=col("eps")).then_inc(setup_act, 1)
            act.wait_ge(setup_act, 3)
            f(col("bn_s", 0, KT), col("bn_s", 0, KT), ACT.Exp, scale=-0.5).then_inc(setup_act, 1)
            act.wait_ge(derived, 1)

            def halo_at(slot, cn, ahead):
                start = (slot + ahead) * (CH * (KC - 1)) + cn * (KC - 1)
                return halo[:, start:start + KC - 1] if isinstance(slot, int) else halo[:, bass.ds(start, KC - 1)]

            def one(i):
                def full(c, name):
                    act.wait_ge(*after("ga_full", i, (c, name)))
                    return ga2[ga_bank((c, name))][:]

                def rstd(c, name, eps, done):
                    f(rs2[:], full(c, name), ACT.Ln, bias=col(eps)).then_inc(sem["ga_evac"], 1)
                    act.wait_ge(*after("ga_evac", i, (c, name)))
                    f(rs2[:], rs2[:], ACT.Exp, scale=-0.5).then_inc(sem[done], 1)

                def mean_copy(name):
                    f(rs2[:], full(1 if name == "mean" else 2, name), ACT.Copy).then_inc(sem["ga_evac"], 1)

                def affine(c):
                    act.wait_ge(*after("yn", i, c))
                    f(yn[:], yn[:], ACT.Identity, scale=col("g1"), bias=col("b1")).then_inc(sem["yn_aff"], 1)

                def late_piece(n):
                    kind, e, m = _late[n]
                    y = full(3, _late[n])
                    if kind == "h":
                        f(hc[:, e, m, :], y, ACT.Identity, bias=col("moe_b1", 2 * e + m)).then_inc(sem["ga_evac"], 1)
                    else:
                        f(late_w[e - 4], y, ACT.Copy).then_inc(sem["ga_evac"], 1)

                def hidden(e, m):
                    f(hc[:, e, m, :], full(2, ("h", e, m)), ACT.Gelu, bias=col("moe_b1", 2 * e + m)).then_inc(sem["ga_evac"], 1)

                def exp(c, u):
                    n = c * UNITS + u
                    if u % 4 == 0:
                        was, back = ((n - RING) // UNITS, 0) if n >= RING else (CH - 1, 1)
                        act.wait_ge(*after("reduced", i, (was, (n - RING) % UNITS // 4), back=back))
                    act.wait_ge(*after("bcast_a", i, (c, u)))
                    f(h[:, n % RING, :], pa[n % 2][:], ACT.Exp, scale=col("A", group(u)[2])).then_inc(sem["exp"], 1)

                for c in range(CH):
                    par, late = (c + 1) % 2, on(LATE[c], i)
                    j, cx = i + (1 if c >= 2 else 0), (c + 2) % CH
                    for u in range(UNITS):
                        if on(0, i):
                            if u == 0:
                                exp(c, 0)
                                exp(c, 1)
                            if u + 2 < UNITS:
                                exp(c, u + 2)
                        if on(prep(c), i) and u == 0:
                            act.wait_ge(*after("conv", i, ((c - 1) % CH, KC - 2), back=1 if c == 0 else 0))
                            act.wait_ge(*after("ga_evac", i, ((c - 1) % CH, "Z"), back=1 if c == 0 else 0))
                            f(ge[:], za[:], ACT.Exp, scale=-1.0).then_inc(sem["neg_exp"], 1)
                        if late and u == {0: 1, 2: 12}.get(c):
                            y = full(c, "outp")
                            f(yn[:], y, ACT.Copy)
                            f(sq2[:, 0, :], y, ACT.Square).then_inc(sem["ga_evac"], 1)
                        if on(prep(c), i) and u == 2:
                            act.wait_ge(*after("cap", i, c))
                            f(ge[:], ge[:], ACT.Ln, bias=col("one")).then_inc(sem["ln_g"], 1)
                        if on(prep(c), i) and u == 3:
                            act.wait_ge(*after("ln_g", i, c))
                            f(ge[:], ge[:], ACT.Exp, scale=-1.0).then_inc(sem["gate"], 1)
                        if late and u == {0: 4, 2: 14}.get(c):
                            rstd(c, "var", "eps", "rstd")
                        if c == 1 and on(1, i) and u in (4, 5):
                            m = u - 4
                            y = full(c, f"wout{m}")
                            f(oc[:, m, :], y, ACT.Identity, scale=col("bn_s", m), bias=col("bn_t", m))
                            f(eo[:, m, :], y, ACT.Exp, scale=col("bn_ns", m), bias=col("bn_nt", m)).then_inc(sem["ga_evac"], 1)
                        if c == 2 and u in (1, 4) and on(0, i):
                            k = u // 4
                            act.wait_ge(*after("xs", i, 0, back=1))
                            f(skip[:, k, :], xs[:, k, :], ACT.Identity, scale=col("skip"), bias=col("b_fc2")).then_inc(sem["skip_in"], 1)
                        if c == 3 and on(1, i) and u - 1 in LATE_SLOTS:
                            late_piece(LATE_SLOTS.index(u - 1))
                        if on(prep(c), i):
                            if u == 6:
                                act.wait_ge(*after("zs", i, c))
                                dt_raw = full(c, "DT")
                                f(v, dt_raw, ACT.Identity, bias=col("b_dt"))
                                f(ev, dt_raw, ACT.Abs, bias=col("b_dt")).then_inc(sem["ga_evac"], 1)
                            if u == 7:
                                f(bs[:, par, :], full(c, "B"), ACT.Copy).then_inc(sem["ga_evac"], 1)
                                act.wait_ge(*after("ga_evac", i, (c, "DT")))
                                f(ev, ev, ACT.Exp, scale=-1.0).then_inc(sem["sp_exp"], 1)
                            if u == 8:
                                f(cs[:, par, :], full(c, "C"), ACT.Copy).then_inc(sem["ga_evac"], 1)
                                act.wait_ge(*after("sp_exp", i, c))
                                f(lnu, ev, ACT.Ln, bias=col("one")).then_inc(sem["sp_ln"], 1)
                        if c == 2 and on(-1, i) and u == 5:
                            mean_copy("hmean")
                        if c == 1 and on(1, i) and u == 14:
                            mean_copy("mean")
                        if c == 2 and on(1, i) and u == 6:
                            y = transposed(ga2[ga_bank((2, "combT"))])
                            full(2, "combT")
                            f(combT[:], y, ACT.Copy)
                            f(combTf[:], y, ACT.Copy).then_inc(sem["ga_evac"], 1)
                        if c == 2 and on(-1, i) and u == 9:
                            act.wait_ge(*after("centred_h", i, 0))
                            f(sq2[:], xn[:], ACT.Square).then_inc(sem["head_sq"], 1)
                        if c == 2 and on(-1, i) and u == 11:
                            rstd(2, "hvar", "head_add", "rstd_h")
                        if c == 1 and on(1, i):
                            if u == 9:
                                act.wait_ge(*after("cap_o", i, 0))
                                f(eo, eo, ACT.Ln, bias=col("one")).then_inc(sem["ln_o"], 1)
                            if u == 10:
                                act.wait_ge(*after("ln_o", i, 0))
                                f(eo, eo, ACT.Exp, scale=-1.0).then_inc(sem["gate_o"], 1)
                        if late and u == 9 and c == 0:
                            affine(c)
                        if c == 2 and u == 13 and on(-1, i):
                            act.wait_ge(*after("xn", i, 0))
                            act.wait_ge(*after("skip_in", i, 1))
                            for k in range(KT):
                                ins = f(xs[:, k, :], xn[:, k, :], ACT.Identity, scale=col("g_head", k), bias=col("b", k))
                            ins.then_inc(sem["xs"], 1)
                        if u == 14 and on(prep(c), i):
                            act.wait_ge(*after("dt", i, c))
                            act.wait_ge(*after("dtx", i, c))
                            f(part[0][:], v2[:], ACT.Copy).then_inc(sem["hi"], 1)
                        if u == 15:
                            if on(prep_in(c), i):
                                x_in = full(c, "X")
                                act.wait_ge(*after("dt", i, c))
                                act.wait_ge(*after("halo", i, (c - 1) % CH, back=1 if c == 0 else 0))
                                f(xh[:, KC - 1:], x_in, ACT.Copy)
                                f(acc, x_in, ACT.Identity, scale=col("conv", KC - 1), bias=col("b_conv"))
                                f(halo_at(j % PER_IMAGE, cx, 1), ga2[ga_bank((c, "X"))][:, T - KC + 1:T], ACT.Copy).then_inc(sem["ga_evac"], 1)
                                f(xh[:, 0:KC - 1], halo_at(j % PER_IMAGE, cx, 0), ACT.Copy).then_inc(sem["halo"], 1)
                            if on(prep_in(c), i):
                                act.wait_ge(*after("dt", i, c))
                                f(zc, full(c, "Z"), ACT.Copy).then_inc(sem["ga_evac"], 1)
                            if on(prep(c), i):
                                act.wait_ge(*after("rest", i, c))
                                f(part[1][:], v2[:], ACT.Copy).then_inc(sem["mid"], 1)
                    if c == 1 and on(1, i):
                        act.wait_ge(*after("centred", i, 0))
                        f(sq2[:], tn[:], ACT.Square).then_inc(sem["tail_sq"], 1)
                        rstd(c, "tvar", "eps", "rstd_t")
                    if late and c in (0, 2):
                        if c == 2:
                            if on(1, i):
                                hidden(0, 0)
                                hidden(0, 1)
                            affine(c)
                            if on(1, i):
                                hidden(1, 0)
                                hidden(1, 1)
                        for hh in range(2):
                            for m in range(2):
                                f(gl[:, hh, m, :], full(c, ("F", hh, m)), ACT.Gelu, bias=col("b_fc1", m)).then_inc(sem["ga_evac"], 1)
                    if c == 1 and on(1, i):
                        y = ga2[ga_bank((1, "router"))][:, 0:4 * NE].rearrange("p (t e) -> p t e", e=NE)
                        full(c, "router")
                        f(lg[:], y, ACT.Copy).then_inc(sem["ga_evac"], 1)
                        act.wait_ge(*after("topk", i, 8))
                        f(pr[:, 1, :], pr[:, 0, :], ACT.Exp).then_inc(sem["topk_exp"], 1)
                    if c == 2 and on(1, i):
                        for _, e, m in _up[2]:
                            if e > 1 or not late:
                                hidden(e, m)
                    if c == 3 and on(1, i):
                        late_piece(10)
                        late_piece(11)
                        for e in range(4, 8):
                            act.wait_ge(*after("ga_evac", i, (3, ("h", e, 1))))
                            f(hc[:, e, :, :], hc[:, e, :, :], ACT.Gelu).then_inc(sem["late_gelu"], 1)
                    if c != 1:
                        act.preload_act_table_set("natural_log_exp_and_others")

            rounds(act, one)

        @block.vector
        def _(dve):
            tt, ts, stt = nc.vector.tensor_tensor, nc.vector.tensor_scalar, nc.vector.scalar_tensor_tensor
            nc.vector.memset(state[:], 0.0)
            nc.vector.memset(halo[:], 0.0)
            nc.vector.memset(col("one"), 1.0)
            nc.vector.memset(col("eps"), LN_EPS)
            nc.vector.memset(col("head_add"), HEAD_ADD).then_inc(ready, 1)
            chain = [0]

            def link(ins):
                chain[0] += 1
                ins.then_inc(setup_dve, 1)
                dve.wait_ge(setup_dve, chain[0])

            dve.wait_ge(ready, READY)
            dve.wait_ge(setup_act, 4)
            link(ts(col("A", 0, UNITS), col("A", 0, UNITS), -1.0, None, ALU.mult))
            link(ts(col("g_head", 0, KT), col("g", 0, KT), HEAD_SCALE, None, ALU.mult))
            link(ts(col("bn_v", 0, KT), col("bn_var", 0, KT), LN_EPS, -0.5, ALU.add, ALU.mult))
            link(tt(col("bn_v", 0, KT), col("bn_v", 0, KT), col("bn_s", 0, KT), ALU.mult))
            link(tt(col("bn_v", 0, KT), col("bn_v", 0, KT), col("bn_s", 0, KT), ALU.mult))
            link(ts(col("bn_v", 0, KT), col("bn_v", 0, KT), 1.5, None, ALU.add))
            link(tt(col("bn_s", 0, KT), col("bn_s", 0, KT), col("bn_v", 0, KT), ALU.mult))
            link(tt(col("bn_s", 0, KT), col("bn_s", 0, KT), col("bn_g", 0, KT), ALU.mult))
            link(tt(col("bn_t", 0, KT), col("bn_s", 0, KT), col("bn_mean", 0, KT), ALU.mult))
            link(tt(col("bn_t", 0, KT), col("bn_b", 0, KT), col("bn_t", 0, KT), ALU.subtract))
            link(ts(col("bn_ns", 0, KT), col("bn_s", 0, KT), -1.0, None, ALU.mult))
            link(ts(col("bn_nt", 0, KT), col("bn_t", 0, KT), -1.0, None, ALU.mult))
            link(nc.vector.reduce_sum(wo_mean[:], wo_s[:], axis=AX_X))
            link(ts(wo_mean[:], wo_mean[:], 1.0 / DM, None, ALU.mult))
            link(ts(wo_s[:], wo_s[:], wo_mean[:, 0:1], None, ALU.subtract))
            dve.sem_inc(derived, 1)

            def state_at(slot, n):
                start = slot * (CH * UNITS) + n
                return state[:, start:start + 1] if isinstance(slot, int) else state[:, bass.ds(start, 1)]

            def one(i):
                def weight(c, u):
                    n = c * UNITS + u
                    dve.wait_ge(*after("bcast_b", i, (c, u)))
                    if u == 0:
                        was = (c - 1) % CH
                        dve.wait_ge(*after("ga_evac", i, (was, "B"), back=1 if c == 0 else 0))
                    was, back = ((n - 3) // UNITS, 0) if n >= 3 else (CH - 1, 1)
                    dve.wait_ge(*after("scan", i, (was, (n - 3) % UNITS), back=back))
                    tt(bx[:, n % 3, :], pb[n % 2][:], bs[:, c % 2, :], ALU.mult).then_inc(sem["bx"], 1)

                def weigh(e):
                    dve.wait_ge(*after("gd_full", i, (2, ("bc", e))))
                    dve.wait_ge(*after("ga_evac", i, (2, ("h", e, 1))))
                    for m in range(2):
                        ins = tt(hc[:, e, m, :], hc[:, e, m, :], gd[:], ALU.mult)
                    ins.then_inc(sem["gd_evac"], 1)

                def finish(c):
                    dve.wait_ge(*after("gd_full", i, (c, "down")))
                    dve.wait_ge(*after("stored", i, c, back=1))
                    if c == 0:
                        dve.wait_ge(*after("fin", i, 0, back=1))
                    tt(fin[:, c, :], fin[:, c, :], gd[:], ALU.add).then_inc(sem["gd_evac"], 1)

                for c in range(CH):
                    par, late = (c + 1) % 2, on(LATE[c], i)
                    for u in range(UNITS):
                        n = c * UNITS + u
                        if c == 0 and on(2, i) and u == 13:
                            finish(c)
                        if on(0, i):
                            if u == 0:
                                weight(c, 0)
                            if u + 1 < UNITS:
                                weight(c, u + 1)
                            dve.wait_ge(*after("exp", i, (c, u)))
                            dve.wait_ge(*after("bx", i, (c, u)))
                            nc.vector.tensor_tensor_scan(h[:, n % RING, :], h[:, n % RING, :], bx[:, n % 3, :], state_at(i % PER_IMAGE, n),
                                                         ALU.mult, ALU.add).then_inc(sem["scan"], 1)
                        if c == 0 and on(2, i) and u in WEIGHT_SLOTS:
                            e = 4 + WEIGHT_SLOTS.index(u)
                            dve.wait_ge(*after("late_gelu", i, e, back=1))
                            w = late_w[e - 4].unsqueeze(1).to_broadcast([P, 2, T])
                            tt(hc[:, e, :, :], hc[:, e, :, :], w, ALU.mult).then_inc(sem["weighted"], 1)
                        if on(prep(c), i):
                            if u == 1:
                                dve.wait_ge(*after("neg_exp", i, c))
                                ts(ge[:], ge[:], EXP_CAP, None, ALU.min).then_inc(sem["cap"], 1)
                            if u == 4:
                                dve.wait_ge(*after("gate", i, c))
                                tt(xcs[:, par, :], acc, ge[:, 1, :], ALU.mult).then_inc(sem["xc"], 1)
                            if u == 7:
                                dve.wait_ge(*after("ga_evac", i, (c, "DT")))
                                ts(v, v, 0.0, None, ALU.max).then_inc(sem["sp_max"], 1)
                            if u == 8:
                                dve.wait_ge(*after("sp_exp", i, c))
                                ts(dr, ev, 1.0, 1.0, ALU.add, ALU.subtract).then_inc(sem["sp_round"], 1)
                            if u == 10:
                                dve.wait_ge(*after("sp_ln", i, c))
                                dve.wait_ge(*after("sp_err", i, c))
                                tt(lnu, lnu, dr, ALU.add).then_inc(sem["sp_sum"], 1)
                            if u == 11:
                                dve.wait_ge(*after("sp_sum", i, c))
                                dve.wait_ge(*after("sp_max", i, c))
                                tt(v2[:, 0, :], lnu, v, ALU.add).then_inc(sem["dt"], 1)
                            if u == 15:
                                dve.wait_ge(*after("hi", i, c))
                                tt(v2[:], v2[:], part[0][:], ALU.subtract).then_inc(sem["rest"], 1)
                        if c == 3 and on(1, i) and u == 0:
                            weigh(3)
                        if late and u == {1: 1, 3: 2}.get(c):
                            pair = 1 if c == 1 else 0
                            dve.wait_ge(*after("gd_full", i, (c, "fc2")))
                            dve.wait_ge(*after("skip_in", i, 1, back=1 if c == 1 else 0))
                            tt(skip[:, pair, :], skip[:, pair, :], gd[:], ALU.add).then_inc(sem["gd_evac"], 1)
                        if c == 1 and on(1, i):
                            if u == 6:
                                dve.wait_ge(*after("ga_evac", i, (1, "wout1")))
                                ts(eo, eo, EXP_CAP, None, ALU.min).then_inc(sem["cap_o"], 1)
                            if u == 11:
                                dve.wait_ge(*after("gate_o", i, 0))
                                tt(oc, oc, eo, ALU.mult).then_inc(sem["o"], 1)
                            if u == 12:
                                dve.wait_ge(*after("o", i, 0))
                                dve.wait_ge(*after("xr", i, 0))
                                tt(x1[:], x1[:], oc, ALU.add).then_inc(sem["x1"], 1)
                            if u == 14:
                                dve.wait_ge(*after("ga_evac", i, (1, "mean")))
                                dve.wait_ge(*after("fin", i, 0, back=1))
                                for m in range(KT):
                                    ins = tt(tn[:, m, :], x1[:, m, :], rs2[:], ALU.subtract)
                                ins.then_inc(sem["centred"], 1)
                        if c == 2 and on(2, i) and u == 5:
                            finish(1)
                        if c == 2 and on(-1, i):
                            if u == 6:
                                dve.wait_ge(*after("ga_evac", i, (2, "hmean")))
                                for m in range(KT):
                                    ins = tt(xn[:, m, :], xn[:, m, :], rs2[:], ALU.subtract)
                                ins.then_inc(sem["centred_h"], 1)
                            if u == 12:
                                dve.wait_ge(*after("rstd_h", i, 0))
                                for m in range(KT):
                                    ins = tt(xn[:, m, :], xn[:, m, :], rs2[:], ALU.mult)
                                ins.then_inc(sem["xn"], 1)
                    if on(prep(c), i):
                        dve.wait_ge(*after("mid", i, c))
                        tt(part[2][:], v2[:], part[1][:], ALU.subtract).then_inc(sem["lo"], 1)
                    for k in range(KC - 1):
                        if on(prep_in(c), i):
                            if k == 0:
                                dve.wait_ge(*after("halo", i, c))
                            else:
                                dve.wait_ge(*after("conv", i, (c, k - 1)))
                            stt(acc, xh[:, k:k + T], col("conv", k), acc, ALU.mult, ALU.add).then_inc(sem["conv"], 1)
                        if k == 1 and c == 1 and on(1, i):
                            dve.wait_ge(*after("rstd_t", i, 0))
                            for m in range(KT):
                                ins = tt(tn[:, m, :], tn[:, m, :], rs2[:], ALU.mult)
                            ins.then_inc(sem["tn"], 1)
                    if on(0, i):
                        dve.wait_ge(*after("reduced", i, (c, 3)))
                        stt(yg[:, c % 2, :], xcs[:, c % 2, :], col("D"), py[:], ALU.mult, ALU.add).then_inc(sem["yd"], 1)
                    if c == 1 and on(1, i):
                        topk(i)
                    if c == 2 and on(1, i):
                        for e in range(3):
                            weigh(e)

            def topk(i):
                step = [0]

                def mark(ins):
                    ins.then_inc(sem["topk"], 1)
                    step[0] += 1

                def then(ins):
                    mark(ins)
                    dve.wait_ge(*after("topk", i, step[0] - 1))

                dve.wait_ge(*after("ga_evac", i, (1, "router")))
                dve.sem_inc(unheeded, 1)
                for t in range(4):
                    mark(nc.vector.max(mx[:, t, :], lg[:, t, :]))
                dve.wait_ge(*after("topk", i, 3))
                dve.sem_inc(unheeded, 1)
                for t in range(4):
                    mark(nc.vector.max_index(ix[:, t, :], mx[:, t, :], lg[:, t, :]))
                mark(tt(pr[:, 0, :], mx[:, :, 1], mx[:, :, 0], ALU.subtract))
                dve.wait_ge(*after("topk", i, 7))
                then(nc.vector.tensor_copy(ixf[:], ix[:, :, 0:2]))
                for k in range(2):
                    mark(tt(cmp[:, k, :, :], iota_s[:], ixf[:, :, k:k + 1].to_broadcast([P, 4, NE]), ALU.is_equal))
                dve.wait_ge(*after("topk_exp", i, 0))
                then(ts(pr[:, 2, :], pr[:, 1, :], 1.0, None, ALU.add))
                then(nc.vector.reciprocal(pr[:, 2, :], pr[:, 2, :]))
                then(tt(pr[:, 3, :], pr[:, 2, :], pr[:, 1, :], ALU.mult))
                mark(tt(cmp[:, 0, :, :], cmp[:, 0, :, :], pr[:, 2, :].unsqueeze(2).to_broadcast([P, 4, NE]), ALU.mult))
                then(tt(cmp[:, 1, :, :], cmp[:, 1, :, :], pr[:, 3, :].unsqueeze(2).to_broadcast([P, 4, NE]), ALU.mult))
                then(tt(comb[:], cmp[:, 0, :, :], cmp[:, 1, :, :], ALU.add))
                then(nc.vector.tensor_copy(c24[:, :, 0:NE], comb[:]))
                then(tt(comb[:], comb[:], c24[:, :, 0:NE], ALU.subtract))
                then(nc.vector.tensor_copy(c24[:, :, NE:2 * NE], comb[:]))
                mark(tt(c24[:, :, 2 * NE:3 * NE], comb[:], c24[:, :, NE:2 * NE], ALU.subtract))
                assert step[0] == TOPK_STEPS

            rounds(dve, one)

        @block.gpsimd
        def _(pool):
            tt = nc.gpsimd.tensor_tensor
            pool.wait_ge(derived, 1)

            def state_at(slot, n):
                start = (slot + 1) * (CH * UNITS) + n
                return state[:, start:start + 4] if isinstance(slot, int) else state[:, bass.ds(start, 4)]

            def one(i):
                for c in range(CH):
                    par, late = (c + 1) % 2, on(LATE[c], i)
                    for u in range(UNITS):
                        n = c * UNITS + u
                        if on(0, i):
                            pool.wait_ge(*after("scan", i, (c, u)))
                            tt(h[:, n % RING, 0:T - 1], h[:, n % RING, 0:T - 1], cs[:, c % 2, 0:T - 1], ALU.mult)
                            if u % 4 == 3:
                                last = h[:, (n - 3) % RING:(n - 3) % RING + 4, T - 1]
                                nc.gpsimd.tensor_copy(state_at(i % PER_IMAGE, n - 3), last).then_inc(sem["saved"], 1)
                                pool.wait_ge(*after("saved", i, (c, u // 4)))
                                tt(last, last, cs[:, c % 2, T - 1:T].to_broadcast([P, 4]), ALU.mult).then_inc(sem["prod"], 1)
                        if on(prep(c), i):
                            if u == 3:
                                pool.wait_ge(*after("gate", i, c))
                                tt(zs[:, par, :], zc, ge[:, 0, :], ALU.mult).then_inc(sem["zs"], 1)
                            if u == 8:
                                pool.wait_ge(*after("sp_round", i, c))
                                tt(dr, ev, dr, ALU.subtract).then_inc(sem["sp_err"], 1)
                            if u == 11:
                                pool.wait_ge(*after("dt", i, c))
                                tt(v2[:, 1, :], v2[:, 0, :], xcs[:, par, :], ALU.mult).then_inc(sem["dtx"], 1)
                        if c == 2 and on(1, i) and u == 8:
                            pool.wait_ge(*after("tn", i, 0))
                            pool.wait_ge(*after("stored", i, 1))
                            tt(fin[:], x1[:], tn[:], ALU.add).then_inc(sem["fin"], 1)
                        if late and u == {0: 5, 2: 15}.get(c):
                            pool.wait_ge(*after("rstd", i, c))
                            tt(yn[:], yn[:], rs2[:], ALU.mult).then_inc(sem["yn"], 1)
                    if on(0, i):
                        pool.wait_ge(*after("yd", i, c))
                        tt(yg[:, c % 2, :], yg[:, c % 2, :], zs[:, c % 2, :], ALU.mult).then_inc(sem["yg"], 1)

            rounds(pool, one)


def kernel(**inputs):
    import ml_dtypes
    import numpy as np
    import concourse.bacc as bacc
    from concourse.bass_utils import run_bass_kernel_spmd

    g = {k: np.asarray(v) for k, v in inputs.items()}
    L0 = {k[len("L0_conv_"):]: v for k, v in g.items() if k.startswith("L0_conv_")}
    FF = {k[len("L0_ffn_"):]: v for k, v in g.items() if k.startswith("L0_ffn_")}
    f32, bf = np.float32, ml_dtypes.bfloat16

    def halves(v):
        return v.reshape(KT, P).T

    def twice(v):
        return np.concatenate([v, v])[:, None]

    small = np.concatenate([
        L0["W_conv"].reshape(DI, KC), L0["b_conv"][:, None], L0["b_dt"][:, None], L0["D_par"][:, None],
        halves(L0["g_norm"]), halves(L0["b_norm"]), twice(L0["g_norm1"]), twice(L0["b_norm1"]),
        L0["b_fc1"].reshape(2, P).T, twice(L0["b_fc2"]), np.broadcast_to(L0["skip_scale"], (P, 1)),
        halves(L0["bn_g"]), halves(L0["bn_b"]), halves(L0["bn_mean"]), halves(L0["bn_var"]),
        FF["b1"].reshape(NE, 2, P).transpose(2, 0, 1).reshape(P, 2 * NE),
        L0["A_log"].reshape(UNITS, P).T], 1)

    def at_half(w):
        o = np.zeros((P, 2, w.shape[1]), w.dtype)
        for k in range(2):
            o[k * DM:(k + 1) * DM, k] = w
        return o

    W_in, Wx = L0["W_in"], L0["W_xproj"]
    wout = L0["W_out"].T.reshape(DM, CH, C).transpose(1, 0, 2).reshape(KT, P, C).transpose(1, 0, 2)
    experts = lambda w: w.reshape(NE, KT, P, C).transpose(2, 0, 1, 3)
    p = np.arange(P)
    red = np.zeros((P, 4, 32), f32)
    sel = np.zeros((PARTS, 32, 4, P), f32)
    for r in range(4):
        red[p, r, 8 * r + p // NS] = 1
        sel[:, 8 * r + p // NS, r, p] = 1
    sele = np.zeros((PARTS, NE, NE, P), f32)
    for e in range(NE):
        sele[:, e, e, :] = 1
    arrays = dict(
        x=g["x"].reshape(B, KT, P, PER_IMAGE, T).transpose(0, 3, 2, 1, 4).reshape(TILES, P, KT, T),
        small=small, wx=at_half(W_in[:DI].T), wz=at_half(W_in[DI:].T), wdtl=Wx[:RK], wdtr=L0["W_dt"].T,
        wb=Wx[RK:RK + NS].T[:, p % NS], wc=Wx[RK + NS:].T[:, p % NS], wo=L0["W_outp"].T,
        wf1=at_half(L0["W_fc1"].T), wf2=L0["W_fc2"].T.reshape(2, P, DM).transpose(1, 0, 2), wout=wout, w1=experts(FF["w1"]), w2=experts(FF["w2"]),
        b2=np.concatenate([FF["b2"]] * PARTS), router=FF["router_w"].T.reshape(KT, P, NE).transpose(1, 0, 2),
        mean256=np.full((P, P), 1 / C, f32), mean64=np.kron(np.eye(2), np.full((DM, DM), 1 / DM)).astype(f32),
        red=red, iota=np.broadcast_to(np.arange(NE, dtype=f32), (P, 4, NE)),
        sel=sel.reshape(PARTS * 32, 4, P).astype(bf), sele=sele.reshape(PARTS * NE, NE, P).astype(bf),
        ident=np.eye(P, dtype=f32).astype(bf))
    arrays = {k: np.ascontiguousarray(v) for k, v in arrays.items()}

    nc = bacc.Bacc("TRN2", target_bir_lowering=False, num_devices=1)
    args = {k: nc.dram_tensor(f"in_{k}", v.shape, mybir.dt.from_np(v.dtype), kind="ExternalInput").ap() for k, v in arrays.items()}
    out = nc.dram_tensor("out_y", (TILES, P, KT, T), F32, kind="ExternalOutput").ap()
    build(nc, **args, out=out)
    r = run_bass_kernel_spmd(nc, [{f"in_{k}": v for k, v in arrays.items()}], core_ids=[0])
    y = np.asarray(r.results[0]["out_y"])
    return y.reshape(B, PER_IMAGE, P, KT, T).transpose(0, 3, 2, 1, 4).reshape(B, C, H, W)
```
